# Optimizing a Trainium2 kernel written in Bass

```python
import numpy as np
import jax
import jax.numpy as jnp

def _softmax(x, axis=-1):
    return jax.nn.softmax(x, axis=axis)

def _gelu(x):
    return jax.nn.gelu(x, approximate=True)

def _silu(x):
    return jax.nn.silu(x)

def _sigmoid(x):
    return jax.nn.sigmoid(x)

def _layernorm(x, axis=-1, eps=1e-05):
    m = jnp.mean(x, axis=axis, keepdims=True)
    v = jnp.var(x, axis=axis, keepdims=True)
    return (x - m) / jnp.sqrt(v + eps)

def _scatter_add(tgt, idx, src, axis=0):
    return tgt.at[idx].add(src)

def _segment_sum(src, seg, n):
    return jax.ops.segment_sum(src, seg, n)
kernel_name = 'mk_cond_seq_d2_seqx_r2_ce546c'

def setup_inputs(seed: int=0):
    np.random.seed(seed)
    _w = jnp.asarray

    def _rec_inputs():
        import jax
        import jax.numpy as jnp
        _rk = jax.random.key(seed)
        x = -0.0003929 + 0.9999 * jax.random.normal(jax.random.fold_in(_rk, 1), (16, 512, 512), jnp.float32)
        _lenS = 512 - jax.random.randint(jax.random.fold_in(_rk, 7), (16,), 0, max(1, 512 // 4) + 1, jnp.int32)
        _lenS2 = 512 - jax.random.randint(jax.random.fold_in(_rk, 8), (16,), 0, max(1, 512 // 4) + 1, jnp.int32)
        cond_2048 = 0.00782532 + 1.00527 * jax.random.normal(jax.random.fold_in(_rk, 11), (16, 1024), jnp.float32)
        _validS = jnp.arange(512)[None, :] < _lenS[:, None]
        _validS2 = jnp.arange(512)[None, :] < _lenS2[:, None]
        _causal = jnp.tril(jnp.ones((512, 512), dtype=bool))
        mask_BxS_ik0 = jnp.where(jnp.broadcast_to(_validS[:, :], (16, 512)), 0, 1).astype(jnp.int32)
        mask_BxSx1_fk1 = jnp.where(jnp.ones((16, 512, 1), dtype=bool), 1.0, 0.0).astype(jnp.float32)
        return (x, cond_2048, mask_BxS_ik0, mask_BxSx1_fk1)
    x, cond_2048, mask_BxS_ik0, mask_BxSx1_fk1 = _rec_inputs()

    def _L0_cond_setup():
        import jax, jax.numpy as jnp
        import numpy as np
        H = 16
        LN_EPS = 1e-05

        def _layernorm(x, scale, bias):
            mu = jnp.mean(x, axis=-1, keepdims=True)
            var = jnp.var(x, axis=-1, keepdims=True)
            return (x - mu) * jax.lax.rsqrt(var + LN_EPS) * scale + bias
        key = jax.random.key(seed)
        ks = jax.random.split(key, 8)
        B, T, D, E = (4, 2048, 512, 1024)
        s = 0.02
        return {'x': jax.random.normal(ks[0], (B, T, D), jnp.float32), 'emb': jax.random.normal(ks[1], (B, E), jnp.float32), 'src_mask': jax.random.randint(ks[2], (B, T), 0, 2).astype(jnp.int32), 'norm_scale': jnp.ones((D,), jnp.float32), 'norm_bias': jnp.zeros((D,), jnp.float32), 'Wq': jax.random.normal(ks[3], (D, D), jnp.float32) * s, 'bq': jnp.zeros((D,), jnp.float32), 'Wk': jax.random.normal(ks[4], (D, D), jnp.float32) * s, 'bk': jnp.zeros((D,), jnp.float32), 'Wv': jax.random.normal(ks[5], (D, D), jnp.float32) * s, 'bv': jnp.zeros((D,), jnp.float32), 'film_emb_W': jax.random.normal(ks[6], (E, 2 * D), jnp.float32) * s, 'film_emb_b': jnp.zeros((2 * D,), jnp.float32), 'film_norm_scale': jnp.ones((D,), jnp.float32), 'film_norm_bias': jnp.zeros((D,), jnp.float32), 'film_out_W': jax.random.normal(ks[7], (D, D), jnp.float32) * s, 'film_out_b': jnp.zeros((D,), jnp.float32)}
    _L0_cond_all = _L0_cond_setup()
    _L0_cond_in = {k: v for k, v in _L0_cond_all.items() if k in ('norm_scale', 'norm_bias', 'Wq', 'bq', 'Wk', 'bk', 'Wv', 'bv', 'film_emb_W', 'film_emb_b', 'film_norm_scale', 'film_norm_bias', 'film_out_W', 'film_out_b')}
    del _L0_cond_all

    def _L1_cond_setup():
        import jax, jax.numpy as jnp
        import numpy as np
        B, T, D, H, TE = (4, 1024, 512, 8, 1024)
        EPS = 1e-05

        def _ln(x, w, b):
            m = jnp.mean(x, axis=-1, keepdims=True)
            v = jnp.mean((x - m) ** 2, axis=-1, keepdims=True)
            return (x - m) * jax.lax.rsqrt(v + EPS) * w + b
        key = jax.random.key(seed)
        ks = jax.random.split(key, 16)
        s = 0.02
        inp = {'x': jax.random.normal(ks[0], (B, T, D), jnp.float32), 'emb': jax.random.normal(ks[1], (B, TE), jnp.float32), 'src_mask': (jax.random.uniform(ks[2], (B, T, 1)) > 0.2).astype(jnp.float32), 'num_head': H, 'ln_w': jnp.ones((D,), jnp.float32), 'ln_b': jnp.zeros((D,), jnp.float32), 'Wq': jax.random.normal(ks[3], (D, D), jnp.float32) * s, 'bq': jnp.zeros((D,), jnp.float32), 'Wk': jax.random.normal(ks[4], (D, D), jnp.float32) * s, 'bk': jnp.zeros((D,), jnp.float32), 'Wv': jax.random.normal(ks[5], (D, D), jnp.float32) * s, 'bv': jnp.zeros((D,), jnp.float32), 'W_emb': jax.random.normal(ks[6], (TE, 2 * D), jnp.float32) * s, 'b_emb': jnp.zeros((2 * D,), jnp.float32), 'ln2_w': jnp.ones((D,), jnp.float32), 'ln2_b': jnp.zeros((D,), jnp.float32), 'W_out': jax.random.normal(ks[7], (D, D), jnp.float32) * s, 'b_out': jnp.zeros((D,), jnp.float32)}
        return inp
    _L1_cond_all = _L1_cond_setup()
    _L1_cond_in = {k: v for k, v in _L1_cond_all.items() if k in ('ln_w', 'ln_b', 'Wq', 'bq', 'Wk', 'bk', 'Wv', 'bv', 'W_emb', 'b_emb', 'ln2_w', 'ln2_b', 'W_out', 'b_out')}
    del _L1_cond_all
    return {'x': x, 'cond_2048': cond_2048, 'mask_BxS_ik0': mask_BxS_ik0, 'mask_BxSx1_fk1': mask_BxSx1_fk1, 'L0_cond_norm_scale': _L0_cond_in['norm_scale'], 'L0_cond_norm_bias': _L0_cond_in['norm_bias'], 'L0_cond_Wq': _L0_cond_in['Wq'], 'L0_cond_bq': _L0_cond_in['bq'], 'L0_cond_Wk': _L0_cond_in['Wk'], 'L0_cond_bk': _L0_cond_in['bk'], 'L0_cond_Wv': _L0_cond_in['Wv'], 'L0_cond_bv': _L0_cond_in['bv'], 'L0_cond_film_emb_W': _L0_cond_in['film_emb_W'], 'L0_cond_film_emb_b': _L0_cond_in['film_emb_b'], 'L0_cond_film_norm_scale': _L0_cond_in['film_norm_scale'], 'L0_cond_film_norm_bias': _L0_cond_in['film_norm_bias'], 'L0_cond_film_out_W': _L0_cond_in['film_out_W'], 'L0_cond_film_out_b': _L0_cond_in['film_out_b'], 'L1_cond_ln_w': _L1_cond_in['ln_w'], 'L1_cond_ln_b': _L1_cond_in['ln_b'], 'L1_cond_Wq': _L1_cond_in['Wq'], 'L1_cond_bq': _L1_cond_in['bq'], 'L1_cond_Wk': _L1_cond_in['Wk'], 'L1_cond_bk': _L1_cond_in['bk'], 'L1_cond_Wv': _L1_cond_in['Wv'], 'L1_cond_bv': _L1_cond_in['bv'], 'L1_cond_W_emb': _L1_cond_in['W_emb'], 'L1_cond_b_emb': _L1_cond_in['b_emb'], 'L1_cond_ln2_w': _L1_cond_in['ln2_w'], 'L1_cond_ln2_b': _L1_cond_in['ln2_b'], 'L1_cond_W_out': _L1_cond_in['W_out'], 'L1_cond_b_out': _L1_cond_in['b_out']}

def reference(x, cond_2048, mask_BxS_ik0, mask_BxSx1_fk1, L0_cond_norm_scale, L0_cond_norm_bias, L0_cond_Wq, L0_cond_bq, L0_cond_Wk, L0_cond_bk, L0_cond_Wv, L0_cond_bv, L0_cond_film_emb_W, L0_cond_film_emb_b, L0_cond_film_norm_scale, L0_cond_film_norm_bias, L0_cond_film_out_W, L0_cond_film_out_b, L1_cond_ln_w, L1_cond_ln_b, L1_cond_Wq, L1_cond_bq, L1_cond_Wk, L1_cond_bk, L1_cond_Wv, L1_cond_bv, L1_cond_W_emb, L1_cond_b_emb, L1_cond_ln2_w, L1_cond_ln2_b, L1_cond_W_out, L1_cond_b_out):
    import jax
    import jax.numpy as jnp

    def _L0_cond_ref(x, emb, src_mask, norm_scale, norm_bias, Wq, bq, Wk, bk, Wv, bv, film_emb_W, film_emb_b, film_norm_scale, film_norm_bias, film_out_W, film_out_b):
        import jax, jax.numpy as jnp
        import numpy as np
        H = 16
        LN_EPS = 1e-05

        def _layernorm(x, scale, bias):
            mu = jnp.mean(x, axis=-1, keepdims=True)
            var = jnp.var(x, axis=-1, keepdims=True)
            return (x - mu) * jax.lax.rsqrt(var + LN_EPS) * scale + bias
        B, T, D = x.shape
        dh = D // H
        xn = _layernorm(x, norm_scale, norm_bias)
        q = xn @ Wq + bq
        k = xn @ Wk + bk
        v = xn @ Wv + bv
        mask = (src_mask == 1)[:, :, None]
        k = jnp.where(mask, -jnp.inf, k)
        v = jnp.where(mask, 0.0, v)
        q = q.reshape(B, T, H, dh).transpose(0, 2, 1, 3)
        k = k.reshape(B, T, H, dh).transpose(0, 2, 1, 3)
        v = v.reshape(B, T, H, dh).transpose(0, 2, 1, 3)
        q = jax.nn.softmax(q, axis=-1)
        k = jax.nn.softmax(k, axis=2)
        attn = jnp.einsum('bhse,bhsd->bhed', k, v)
        y = jnp.einsum('bhtd,bhed->bhte', q, attn)
        y = y.transpose(0, 2, 1, 3).reshape(B, T, D)
        emb_out = jax.nn.silu(emb) @ film_emb_W + film_emb_b
        scale, shift = jnp.split(emb_out, 2, axis=-1)
        h = _layernorm(y, film_norm_scale, film_norm_bias) * (1.0 + scale[:, None, :]) + shift[:, None, :]
        h = jax.nn.silu(h) @ film_out_W + film_out_b
        return x + h

    def _L1_cond_ref(x, emb, src_mask, num_head, ln_w, ln_b, Wq, bq, Wk, bk, Wv, bv, W_emb, b_emb, ln2_w, ln2_b, W_out, b_out):
        import jax, jax.numpy as jnp
        import numpy as np
        B, T, D, H, TE = (4, 1024, 512, 8, 1024)
        EPS = 1e-05

        def _ln(x, w, b):
            m = jnp.mean(x, axis=-1, keepdims=True)
            v = jnp.mean((x - m) ** 2, axis=-1, keepdims=True)
            return (x - m) * jax.lax.rsqrt(v + EPS) * w + b
        b, t, d = x.shape
        h = num_head
        dh = d // h
        xn = _ln(x, ln_w, ln_b)
        q = xn @ Wq + bq
        k = xn @ Wk + bk + (1.0 - src_mask) * -1000000.0
        q = jax.nn.softmax(q.reshape(b, t, h, dh), axis=-1)
        k = jax.nn.softmax(k.reshape(b, t, h, dh), axis=1)
        v = ((xn @ Wv + bv) * src_mask).reshape(b, t, h, dh)
        att = jnp.einsum('bnhd,bnhl->bhdl', k, v)
        y = jnp.einsum('bnhd,bhdl->bnhl', q, att).reshape(b, t, d)
        emb_out = (jax.nn.silu(emb) @ W_emb + b_emb)[:, None, :]
        scale, shift = jnp.split(emb_out, 2, axis=2)
        hh = _ln(y, ln2_w, ln2_b) * (1.0 + scale) + shift
        hh = jax.nn.silu(hh) @ W_out + b_out
        return x + hh
    x = _L0_cond_ref(x, cond_2048, mask_BxS_ik0, L0_cond_norm_scale, L0_cond_norm_bias, L0_cond_Wq, L0_cond_bq, L0_cond_Wk, L0_cond_bk, L0_cond_Wv, L0_cond_bv, L0_cond_film_emb_W, L0_cond_film_emb_b, L0_cond_film_norm_scale, L0_cond_film_norm_bias, L0_cond_film_out_W, L0_cond_film_out_b)
    x = _L1_cond_ref(x, cond_2048, mask_BxSx1_fk1, 8, L1_cond_ln_w, L1_cond_ln_b, L1_cond_Wq, L1_cond_bq, L1_cond_Wk, L1_cond_bk, L1_cond_Wv, L1_cond_bv, L1_cond_W_emb, L1_cond_b_emb, L1_cond_ln2_w, L1_cond_ln2_b, L1_cond_W_out, L1_cond_b_out)
    return x

_drawn_inputs = setup_inputs


def setup_inputs(seed=0):
    import zlib

    import numpy as np

    out = dict(_drawn_inputs(seed))
    spreads = {'L0_cond_norm_scale': (1.0, 0.2),
     'L0_cond_norm_bias': (0.0, 0.1),
     'L0_cond_bq': (0.0, 0.1),
     'L0_cond_bk': (0.0, 0.8),
     'L0_cond_bv': (0.0, 0.1),
     'L0_cond_film_emb_b': (0.0, 0.1),
     'L0_cond_film_norm_scale': (1.0, 0.2),
     'L0_cond_film_norm_bias': (0.0, 0.1),
     'L0_cond_film_out_b': (0.0, 0.1),
     'L1_cond_ln_w': (1.0, 0.2),
     'L1_cond_ln_b': (0.0, 0.1),
     'L1_cond_bq': (0.0, 0.8),
     'L1_cond_bk': (0.0, 0.8),
     'L1_cond_bv': (0.0, 0.1),
     'L1_cond_b_emb': (0.0, 0.1),
     'L1_cond_ln2_w': (1.0, 0.2),
     'L1_cond_ln2_b': (0.0, 0.287),
     'L1_cond_b_out': (0.0, 0.1)}
    factors = {'L1_cond_Wq': 8.0, 'L1_cond_Wk': 8.0}
    for name, (base, spread) in spreads.items():
        noise = np.random.default_rng([zlib.crc32(name.encode()), seed]).standard_normal(out[name].shape)
        drawn = base * np.exp(spread * noise) if base else spread * noise
        out[name] = jnp.asarray(drawn.astype(out[name].dtype))
    for name, factor in factors.items():
        out[name] = (out[name] * factor).astype(out[name].dtype)
    return out
```

```python
from contextlib import ExitStack

import concourse.bass as bass
from concourse import mybir

F32, F16, BF16, I32 = mybir.dt.float32, mybir.dt.float16, mybir.dt.bfloat16, mybir.dt.int32
ALU = mybir.AluOpType
ACT = mybir.ActivationFunctionType
AX = mybir.AxisListType

P = 128
B, T, D, E = 16, 512, 512, 1024
NT, NC, NE = T // P, D // P, E // P
HEADS = (16, 8)
EPS = 1e-5
XS = 2048.0
PS = 16384.0
ROOT = 22.63
MASKED = -3.0e38
WK, WQ, WV, WO = range(4)
HI, LO = 0, 1
G, LNB, FS, FB, BK, BE = 0, 4, 8, 12, 16, 20
NV = 28
PRODUCTS = ((HI, HI), (HI, LO), (LO, HI))
PROJ, TR, TAIL = 0, 3, 5


def build(nc, x, cond, mask0, mask1, w, vec, out):
    with ExitStack() as ctx:
        def sb(name, shape, dt):
            return ctx.enter_context(nc.sbuf_tensor(name, shape, dt))

        def sem(name):
            return ctx.enter_context(nc.semaphore(name))

        wsp = [sb(f"wsp{L}", [P, 4, 2, NC, D], F16) for L in range(2)]
        xin = [sb(f"xin{L}", [P, NT, D], F32) for L in range(2)]
        xr = [sb(f"xr{L}", [P, NT, D], F32) for L in range(2)]
        xh = sb("xh", [P, NT, D], F32)
        yh = sb("yh", [P, NT, D], F32)
        xT = sb("xT", [P, 2, NC, T], F16)
        kf = sb("kf", [P, NC, T], F32)
        qf = sb("qf", [P, NT, D], F32)
        Ks = sb("Ks", [P, 2, NT, D], F16)
        Vs = sb("Vs", [P, 2, NT, D], F16)
        qT = sb("qT", [P, 2, NC, T], F16)
        hT = sb("hT", [P, 2, NC, T], F16)
        af = sb("af", [P, D], F32)
        As = sb("As", [P, 2, D], F16)
        vtmp = sb("vtmp", [P, 2, D], F32)
        z = sb("z", [P, 3, T], F32)
        th = sb("th", [P, 2, T], F32)
        madd = sb("madd", [P, T], F32)
        bc = [sb(f"bc{L}", [P, 3, D], F32) for L in range(2)]
        diag = [sb(f"diag{L}", [P, D], BF16) for L in range(2)]
        ident = sb("ident", [P, P], F32)
        rows = sb("rows", [2 * NV, P], F32)
        cols = sb("cols", [P, 2 * NV], F32)
        embT = sb("embT", [P, NE, B], F32)
        tab = [sb(f"tab{L}", [P, B, 12], F32) for L in range(2)]
        film_t = sb("film_t", [P, 2, NC, B], F32)
        vms = sb("vms", [P, NT], F32)
        ghs = sb("ghs", [P, 8], F32)
        sc = [sb(f"sc{L}", [P, 40], F32) for L in range(2)]
        gs = sb("gs", [P, 4, NC], F32)
        gabs = sb("gabs", [P, NC], F32)
        kam = sb("kam", [P, 2, NC], F32)
        bkp = sb("bkp", [P, 2, NC], F32)
        kbias = sb("kbias", [P, NC], F32)
        nan0 = sb("nan0", [P, 2], F32)
        nkmax = sb("nkmax", [P, NC], F32)
        ksum = sb("ksum", [P, NC], F32)
        rk = sb("rk", [P, NC], F32)
        nqmax = sb("nqmax", [P, NT, 16], F32)
        qsum = sb("qsum", [P, NT, 16], F32)
        rq = sb("rq", [P, NT, 16], F32)
        xbs = sb("xbs", [P, NT, 6], F32)
        xmv = sb("xmv", [P, NT, 2], F32)
        xvar = sb("xvar", [P, NT], F32)
        xr_std = sb("xr_std", [P, NT], F32)
        ybs = sb("ybs", [P, NT, 6], F32)
        ymv = sb("ymv", [P, NT, 2], F32)
        yvar = sb("yvar", [P, NT], F32)
        yr_std = sb("yr_std", [P, NT], F32)
        ynb = sb("ynb", [P, NT], F32)
        mhalf = sb("mhalf", [P, NT], F32)
        ps = ctx.enter_context(nc.psum_tensor("ps", [P, 8, 512], F32))

        AM, AR, S, INV = 0, 6, 12, 18
        CK, CQ, CV, CO, EPSY = 24, 25, 26, 27, 28
        TMP = 30
        FILM, VAL = 4, 5

        def raw(m):
            return wsp[1][:, m].rearrange("p a k n -> p (a k n)").bitcast(F32).rearrange("p (k n) -> p k n", k=NC)

        stage = (xr[1][:, :, :], xin[1][:, :, :])

        def wraw(L, m):
            return raw(m) if L == 0 else stage[m % 2]

        def quarter(i):
            return stage[i % 2].rearrange("p t n -> p (t n)").rearrange("p (k n) -> p k n", k=NE)

        s_x, s_rows, s_bc, s_small, s_mask, s_zero = sem("s_x"), sem("s_rows"), sem("s_bc"), sem("s_small"), sem("s_mask"), sem("s_zero")
        s_w0 = [sem(f"s_w0_{m}") for m in range(4)]
        s_stage = [sem("s_stageA"), sem("s_stageB")]
        s_store = [sem(f"s_store{t}") for t in range(NT)]
        pool_const, dve_pro, act_pro, pool_pro, pe_pro = sem("pool_const"), sem("dve_pro"), sem("act_pro"), sem("pool_pro"), sem("pe_pro")
        pe_bias, pe_film, act_whi, dve_wlo, dve_film = sem("pe_bias"), sem("pe_film"), sem("act_whi"), sem("dve_wlo"), sem("dve_film")
        dve_am, pool_am, dve_scale, dve_bias = sem("dve_am"), sem("pool_am"), sem("dve_scale"), sem("dve_bias")
        dve_prep = sem("dve_prep")
        pe_xt, pe_k, pe_q, pe_v, pe_kt, pe_qt = (sem(f"pe_{n}") for n in ("xt", "k", "q", "v", "kt", "qt"))
        pe_at, pe_y, pe_yt, pe_o = (sem(f"pe_{n}") for n in ("at", "y", "yt", "o"))
        act_xhi, act_kf, act_ke, act_khi, act_qe, act_qhi, act_vhi = (sem(f"act_{n}") for n in ("xhi", "kf", "ke", "khi", "qe", "qhi", "vhi"))
        act_ahi, act_yh, act_z, act_th, act_hhi = (sem(f"act_{n}") for n in ("ahi", "yh", "z", "th", "hhi"))
        dve_xst, dve_xag, dve_xvar, dve_xh, dve_xlo = (sem(f"dve_{n}") for n in ("xst", "xag", "xvar", "xh", "xlo"))
        dve_kmax, dve_ksum, dve_klo, dve_kb, dve_kb1 = (sem(f"dve_{n}") for n in ("kmax", "ksum", "klo", "kb", "kb1"))
        dve_q, dve_qmax, dve_qs, dve_rq, dve_qlo = (sem(f"dve_{n}") for n in ("q", "qmax", "qs", "rq", "qlo"))
        dve_v, dve_vlo, dve_af, dve_alo = (sem(f"dve_{n}") for n in ("v", "vlo", "af", "alo"))
        dve_yst, dve_yag, dve_yvar, dve_ynb = (sem(f"dve_{n}") for n in ("yst", "yag", "yvar", "ynb"))
        dve_h, dve_o = sem("dve_h"), sem("dve_o")
        pool_vm, pool_gh, pool_km, pool_kn, pool_qs, pool_qn, pool_xr, pool_xstd, pool_ystd, pool_madd, pool_hlo = (
            sem(f"pool_{n}") for n in ("vm", "gh", "km", "kn", "qs", "qn", "xr", "xstd", "ystd", "madd", "hlo"))

        def c1(L, j):
            return sc[L][:, j:j + 1]

        def heads(ap, L):
            return ap.rearrange("p (h e) -> p h e", h=HEADS[L])

        def per_head(ap, L):
            return ap[:, 0:HEADS[L]].rearrange("p (h e) -> p h e", e=1).to_broadcast((P, HEADS[L], D // HEADS[L]))

        x_rows = x.rearrange("b (t p) d -> b p t d", p=P)
        out_rows = out.rearrange("b (t p) d -> b p t d", p=P)

        def reused(u, n):
            return not (isinstance(u, int) and u < n)

        def count(eng, n):
            return n if isinstance(n, int) else eng.snap(eng.to_reg(n))

        block = ctx.enter_context(nc.Block())

        @block.sync
        def _(sp):
            for t in range(NT):
                sp.sem_inc(s_store[t], 16)
            sp.dma_start(xin[0][:, :, :], x_rows[0]).then_inc(s_x, 16)
            for L in range(2):
                r = NV * L
                for name, n in (("g", 4), ("lnb", 4), ("fs", 4), ("fb", 4), ("bk", 4), ("be", 8)):
                    sp.dma_start(rows[r:r + n, :], vec[L][name].rearrange("(r p) -> r p", p=P)).then_inc(s_rows, 16)
                    r += n
            for m in range(4):
                sp.dma_start(raw(m), w[0][m].rearrange("(k p) n -> p k n", p=P)).then_inc(s_w0[m], 16)
                if m == 0:
                    sp.dma_start(vtmp[0:B, 0, :].bitcast(I32), mask0).then_inc(s_small, 16)
                    sp.dma_start(vtmp[0:B, 1, :], mask1).then_inc(s_small, 16)
                    sp.dma_start(z[0:B, 0:2, :].rearrange("p a n -> p (a n)"), cond).then_inc(s_small, 16)
                    sp.dma_start(madd[:, :].bitcast(I32), mask0[0:1, :].to_broadcast((P, T))).then_inc(s_mask, 16)
                    for L in range(2):
                        for j, name in enumerate(("bq", "bv", "bo")):
                            sp.dma_start(bc[L][:, j, :], vec[L][name].rearrange("(a n) -> a n", a=1).to_broadcast((P, D))).then_inc(s_bc, 16)

            def load_mask(u, L, b, tests):
                n0 = count(sp, 4 * u)
                n1 = count(sp, tests)
                sp.wait_ge(s_rows, 16 * 12)
                sp.wait_ge(pool_km, n0)
                sp.wait_ge(dve_kb, n1)
                if L == 1:
                    sp.dma_start(madd[:, :], mask1[bass.ds(b, 1), :].to_broadcast((P, T))).then_inc(s_mask, 16)
                else:
                    sp.dma_start(madd[:, :].bitcast(I32), mask0[bass.ds(b, 1), :].to_broadcast((P, T))).then_inc(s_mask, 16)

            def load_x(b, before):
                n0 = count(sp, 4 * before + 4)
                n1 = count(sp, 4 * before + 4)
                sp.wait_ge(s_rows, 16 * 12)
                sp.wait_ge(dve_xh, n0)
                sp.wait_ge(pool_xr, n1)
                sp.dma_start(xin[0][:, :, :], x_rows[b]).then_inc(s_x, 16)

            def load_stage(j):
                k = j - 2
                if 0 <= k < 4:
                    sp.wait_ge(pe_film, k + 1)
                elif 4 <= k < 8:
                    sp.wait_ge(act_whi, k + 1)
                    sp.wait_ge(dve_wlo, k + 1)
                    if k < 7:
                        sp.wait_ge(pe_bias, k)
                elif k >= 8:
                    sp.wait_ge(pe_film, k - 3)
                if 4 <= j < 8:
                    sp.dma_start(stage[j % 2], w[1][j - 4].rearrange("(k p) n -> p k n", p=P)).then_inc(s_stage[j % 2], 16)
                else:
                    L, q = (0, j) if j < 4 else (1, j - 8)
                    sp.dma_start(quarter(j), w[L][4].rearrange("(k p) n -> p k n", p=P)[:, :, 256 * q:256 * q + 256]).then_inc(s_stage[j % 2], 16)

            load_stage(0)
            load_stage(1)
            load_x(1, 0)
            load_mask(1, 0, 1, 1)
            for j in range(2, 12):
                load_stage(j)
            load_mask(2, 1, 0, 2)

            def store(b, u):
                for t in range(NT):
                    n = count(sp, 4 * u + t + 1)
                    sp.wait_ge(s_rows, 16 * 12)
                    sp.wait_ge(dve_o, n)
                    sp.dma_start(out_rows[b][:, t, :], xr[1][:, t, :]).then_inc(s_store[t], 16)

            with sp.Fori(1, B - 1) as i:
                load_x(i + 1, 2 * i - 1)
                load_mask(2 * i + 1, 0, i + 1, i + 1)
                load_mask(2 * i + 2, 1, i, i + 2)
                store(i - 1, 2 * i)
            load_mask(31, 1, 15, 16)
            store(14, 30)
            store(15, 31)
            for t in range(NT):
                sp.wait_ge(s_store[t], 16 * (B + 1))

        @block.gpsimd
        def _(pool):
            def tt(o, a, b, op):
                return nc.gpsimd.tensor_tensor(o, a, b, op)

            pool.memset(ident[:, :], 0.0).then_inc(pool_const, 1)
            pool.memset(mhalf[:, :], -0.5).then_inc(pool_const, 1)
            for L in range(2):
                pool.memset(diag[L][:, :], 1.0).then_inc(pool_const, 1)
            pool.wait_ge(pool_const, 4)
            pool.affine_select(out=ident[:, :], in_=ident[:, :], compare_op=ALU.not_equal, fill=1.0, base=0,
                               pattern=[[-1, P]], channel_multiplier=1).then_inc(pool_const, 1)
            n = 5
            for L in range(2):
                hd = D // HEADS[L]
                v = diag[L][:, :].rearrange("p (c h e) -> p c h e", c=NC, e=hd)
                pool.affine_select(out=v, in_=v, compare_op=ALU.is_ge, fill=0.0, base=0,
                                   pattern=[[0, NC], [-hd, P // hd], [0, hd]], channel_multiplier=1).then_inc(pool_const, 1)
                n += 1
                pool.wait_ge(pool_const, n)
                pool.affine_select(out=v, in_=v, compare_op=ALU.is_ge, fill=0.0, base=hd - 1,
                                   pattern=[[0, NC], [hd, P // hd], [0, hd]], channel_multiplier=-1).then_inc(pool_const, 1)
                n += 1

            def bounds(L, js):
                for j in js:
                    pool.wait_ge(dve_am, 5 * L + j + 1)
                    pool.partition_all_reduce(c1(L, AR + j), c1(L, AM + j), P, bass.bass_isa.ReduceOp.max).then_inc(pool_am, 1)

            def mask_add(u, L):
                n = count(pool, 16 * (u + 1))
                pool.wait_ge(pool_const, 4)
                pool.wait_ge(s_mask, n)
                if L == 0:
                    pool.tensor_scalar(madd[:, :], madd[:, :].bitcast(I32), 1.0, MASKED, ALU.is_equal, ALU.mult).then_inc(pool_madd, 1)
                else:
                    pool.tensor_scalar(madd[:, :], madd[:, :], 1.0, 1.0e6, ALU.subtract, ALU.mult).then_inc(pool_madd, 1)

            def x_std(u):
                pool.wait_ge(dve_xvar, u + 1)
                tt(xr_std[:, :], xvar[:, :], mhalf[:, :], ALU.pow).then_inc(pool_xstd, 1)

            def prepare(u, L, b):
                x_std(u)
                mask_add(u, L)

            def residual(u, L, b, t):
                if L == 1:
                    pool.wait_ge(s_store[t], 16 * (b + 1))
                tt(xr[L][:, t, :], xin[L][:, t, :], bc[L][:, 2, :], ALU.add).then_inc(pool_xr, 1)

            def step(u, A, Bu, N, between=None):
                late = Bu is not None and A is not None and A[0] == Bu[0]
                u_is_0 = Bu is None
                v = u - 1

                def key_mask(c):
                    pool.wait_ge(act_kf, 4 * u + c + 1)
                    if c == 0:
                        pool.wait_ge(pool_madd, u + 1)
                    tt(kf[:, c, :], kf[:, c, :], madd[:, :], ALU.add).then_inc(pool_km, 1)

                def key_norm(c):
                    if c == 0:
                        n = count(pool, u + 1)
                        pool.wait_ge(pool_const, 4)
                        pool.wait_ge(dve_ksum, n)
                    pool.tensor_scalar(kf[:, c, :], kf[:, c, :], rk[:, c:c + 1], PS, ALU.mult, ALU.mult).then_inc(pool_kn, 1)

                def query_shift(t):
                    pool.wait_ge(dve_qmax, 4 * u + t + 1)
                    tt(heads(qf[:, t, :], A[0]), heads(qf[:, t, :], A[0]), per_head(nqmax[:, t], A[0]), ALU.add).then_inc(pool_qs, 1)

                def query_norm(t):
                    pool.wait_ge(dve_rq, 4 * u + t + 1)
                    pool.wait_ge(act_qe, 4 * u + t + 1)
                    tt(heads(qf[:, t, :], A[0]), heads(qf[:, t, :], A[0]), per_head(rq[:, t], A[0]), ALU.mult).then_inc(pool_qn, 1)

                def h_lo(c):
                    pool.wait_ge(act_hhi, 4 * v + c + 1)
                    tt(hT[:, LO, c, :], z[:, c % 3, :], hT[:, HI, c, :], ALU.subtract).then_inc(pool_hlo, 1)

                def y_std(t):
                    pool.wait_ge(dve_yvar, 4 * v + t + 1)
                    tt(yr_std[:, t:t + 1], yvar[:, t:t + 1], mhalf[:, 0:1], ALU.pow).then_inc(pool_ystd, 1)

                if A:
                    if u_is_0:
                        pool.wait_ge(dve_prep, 1)
                        pool.wait_ge(s_bc, 16 * 6)
                    else:
                        pool.wait_ge(dve_prep, A[0] + 1)
                        pool.wait_ge(act_vhi, 4 * u)
                        pool.wait_ge(dve_vlo, 4 * u)
                    pool.tensor_copy(vms[:, :], tab[A[0]][:, bass.ds(A[1], 1), 0:4].rearrange("p a c -> p (a c)")).then_inc(pool_vm, 1)
                if Bu:
                    pool.wait_ge(dve_film, Bu[0] + 1)
                    if reused(u, 2):
                        pool.wait_ge(act_z, 4 * v)
                    pool.tensor_copy(ghs[:, :], tab[Bu[0]][:, bass.ds(Bu[1], 1), 4:12].rearrange("p a c -> p (a c)")).then_inc(pool_gh, 1)
                if A:
                    if A[0] == 0:
                        pool.wait_ge(s_x, 16 * (A[1] + 1))
                    if reused(u, 2) and not late:
                        pool.wait_ge(dve_o, 4 * v)
                    key_mask(0)
                    if not late:
                        residual(u, *A, 0)
                        residual(u, *A, 1)
                    key_mask(1)
                if Bu:
                    y_std(0)
                if A:
                    if not late:
                        residual(u, *A, 2)
                    key_mask(2)
                if Bu:
                    y_std(1)
                if A:
                    if N:
                        x_std(u + 1)
                    key_mask(3)
                if Bu:
                    y_std(2)
                if A:
                    if not late:
                        residual(u, *A, 3)
                if Bu:
                    y_std(3)
                if A:
                    query_shift(0)
                    key_norm(0)
                    key_norm(1)
                    query_shift(1)
                    key_norm(2)
                    query_norm(0)
                    query_shift(2)
                    key_norm(3)
                    query_norm(1)
                    query_shift(3)
                if Bu:
                    h_lo(0)
                    h_lo(1)
                if A:
                    query_norm(2)
                    query_norm(3)
                if Bu:
                    h_lo(2)
                    h_lo(3)
                if A:
                    if N:
                        mask_add(u + 1, N[0])
                    if between:
                        between()
                    if late:
                        pool.wait_ge(dve_o, 4 * u)
                        for t in range(NT):
                            residual(u, *A, t)

            prepare(0, 0, 0)
            bounds(0, (0, 1, 2))
            step(0, (0, 0), None, None)
            bounds(0, (3, 4))
            prepare(1, 0, 1)
            step(1, (0, 1), (0, 0), None, between=lambda: bounds(1, (0, 1, 2, 3, 4)))
            prepare(2, 1, 0)
            with pool.Fori(1, B - 1) as i:
                step(2 * i, (1, i - 1), (0, i), (0, i + 1))
                step(2 * i + 1, (0, i + 1), (1, i - 1), (1, i))
            step(30, (1, 14), (0, 15), None)
            prepare(31, 1, 15)
            step(31, (1, 15), (1, 14), None)
            step(32, None, (1, 15), None)

        @block.scalar
        def _(act):
            def split_weights(L, ms):
                for m in ms:
                    act.wait_ge(dve_scale, 4 * L + m + 1)
                    if L == 1:
                        act.wait_ge(pe_bias, 3)
                        act.wait_ge(dve_wlo, 4)
                    for k in range(NC):
                        last = nc.scalar.activation(wsp[L][:, m, HI, k, :], wraw(L, m)[:, k, :], ACT.Copy, scale=gs[:, m, k:k + 1])
                    last.then_inc(act_whi, 1)

            def prepare(u):
                for j in range(NC):
                    act.wait_ge(pe_xt, 4 * u + j + 1)
                    if j == 0 and reused(u, 1):
                        act.wait_ge(pe_v, 4 * u)
                    nc.scalar.activation(xT[:, HI, j, :], ps[:, TR + j % 2, :], ACT.Copy).then_inc(act_xhi, 1)

            def step(u, A, Bu, N, between=None):
                v = u - 1

                def keys(c):
                    act.wait_ge(pe_k, 4 * u + c + 1)
                    if c == 0:
                        act.wait_ge(dve_prep, A[0] + 1)
                        if A[0] == 0:
                            act.wait_ge(dve_kb, A[1] + 1)
                        if Bu:
                            act.wait_ge(pe_kt, 4 * u)
                    bias = kbias if A[0] == 0 else bkp[:, 1]
                    nc.scalar.activation(kf[:, c, :], ps[:, PROJ + c % 3, :], ACT.Identity, bias=bias[:, c:c + 1],
                                         scale=c1(A[0], CK)).then_inc(act_kf, 1)

                def key_exp(c):
                    act.wait_ge(dve_kmax, 4 * u + c + 1)
                    nc.scalar.activation(kf[:, c, :], kf[:, c, :], ACT.Exp, bias=nkmax[:, c:c + 1],
                                         accum_out=ksum[:, c:c + 1]).then_inc(act_ke, 1)

                def y_norm(t):
                    act.wait_ge(dve_ynb, 4 * v + t + 1)
                    if t == 0 and reused(u, 2):
                        act.wait_ge(pe_yt, 4 * v)
                    nc.scalar.activation(yh[:, t, :], ps[:, TAIL + (1 + t) % 3, :], ACT.Identity, bias=ynb[:, t:t + 1],
                                         scale=yr_std[:, t:t + 1]).then_inc(act_yh, 1)

                def query_exp(t):
                    act.wait_ge(pool_qs, 4 * u + t + 1)
                    nc.scalar.activation(qf[:, t, :], qf[:, t, :], ACT.Exp).then_inc(act_qe, 1)

                def film_in(c):
                    act.wait_ge(pe_yt, 4 * v + c + 1)
                    if c == 0:
                        act.wait_ge(pool_gh, v + 1)
                    if c == 3 or reused(u, 2):
                        act.wait_ge(pool_hlo, 4 * v + (1 if c == 3 else 0))
                    nc.scalar.activation(z[:, c % 3, :], ps[:, TR + c % 2, :], ACT.Identity, bias=ghs[:, 4 + c:5 + c],
                                         scale=ghs[:, c:c + 1]).then_inc(act_z, 1)

                def tanh(c):
                    act.wait_ge(act_z, 4 * v + c + 1)
                    if c >= 2 or reused(u, 2):
                        act.wait_ge(dve_h, 4 * v + c - 1)
                    nc.scalar.activation(th[:, c % 2, :], z[:, c % 3, :], ACT.Tanh, scale=c1(Bu[0], INV + FILM)).then_inc(act_th, 1)

                def h_hi(c):
                    act.wait_ge(dve_h, 4 * v + c + 1)
                    if c == 0 and reused(u, 2):
                        act.wait_ge(pe_o, 4 * v)
                    nc.scalar.activation(hT[:, HI, c, :], z[:, c % 3, :], ACT.Copy).then_inc(act_hhi, 1)

                def k_hi(t):
                    act.wait_ge(pe_kt, 4 * u + t + 1)
                    nc.scalar.activation(Ks[:, HI, t, :], ps[:, TR + t % 2, :], ACT.Copy).then_inc(act_khi, 1)

                def v_hi(t):
                    act.wait_ge(dve_v, 4 * u + t + 1)
                    if t == 0:
                        act.wait_ge(pool_vm, u + 1)
                        if Bu:
                            act.wait_ge(pe_at, u)
                    nc.scalar.activation(Vs[:, HI, t, :], vtmp[:, t % 2, :], ACT.Copy, scale=vms[:, t:t + 1]).then_inc(act_vhi, 1)

                def q_hi(c):
                    act.wait_ge(pe_qt, 4 * u + c + 1)
                    if c == 0 and Bu:
                        act.wait_ge(pe_y, 4 * u)
                    nc.scalar.activation(qT[:, HI, c, :], ps[:, TR + c % 2, :], ACT.Copy, scale=PS).then_inc(act_qhi, 1)

                if A:
                    keys(0)
                if Bu:
                    act.wait_ge(dve_af, v + 1)
                    if reused(u, 2):
                        act.wait_ge(pe_y, 4 * v)
                    nc.scalar.activation(As[:, HI, :], af[:, :], ACT.Copy).then_inc(act_ahi, 1)
                if A:
                    key_exp(0)
                    keys(1)
                    key_exp(1)
                    keys(2)
                if Bu:
                    y_norm(0)
                if A:
                    key_exp(2)
                    keys(3)
                if Bu:
                    y_norm(1)
                    y_norm(2)
                if A:
                    key_exp(3)
                if Bu:
                    y_norm(3)
                if A:
                    query_exp(0)
                    query_exp(1)
                if Bu:
                    film_in(0)
                    film_in(1)
                if A:
                    query_exp(2)
                if Bu:
                    tanh(0)
                    tanh(1)
                    film_in(2)
                if A:
                    query_exp(3)
                if Bu:
                    h_hi(0)
                    h_hi(1)
                if A:
                    v_hi(0)
                if Bu:
                    film_in(3)
                if A:
                    k_hi(0)
                    k_hi(1)
                    v_hi(1)
                if Bu:
                    tanh(2)
                    tanh(3)
                if A:
                    k_hi(2)
                    k_hi(3)
                if Bu:
                    h_hi(2)
                    h_hi(3)
                if A:
                    v_hi(2)
                    q_hi(0)
                    q_hi(1)
                    v_hi(3)
                    if between:
                        between()
                    q_hi(2)
                    q_hi(3)
                    if N:
                        prepare(u + 1)

            act.wait_ge(dve_pro, 2)
            nc.scalar.activation(th[0:B, :, :].rearrange("p a n -> p (a n)"), z[0:B, 0:2, :].rearrange("p a n -> p (a n)"),
                                 ACT.Tanh).then_inc(act_pro, 1)
            prepare(0)
            split_weights(0, (WK, WQ, WV))
            step(0, (0, 0), None, None)
            split_weights(0, (WO,))
            prepare(1)
            step(1, (0, 1), (0, 0), None, between=lambda: split_weights(1, (WK, WQ, WV, WO)))
            prepare(2)
            with act.Fori(1, B - 1) as i:
                step(2 * i, (1, i - 1), (0, i), (0, i + 1))
                step(2 * i + 1, (0, i + 1), (1, i - 1), (1, i))
            step(30, (1, 14), (0, 15), None)
            prepare(31)
            step(31, (1, 15), (1, 14), None)
            step(32, None, (1, 15), None)

        @block.vector
        def _(dve):
            ts, stt, tt = nc.vector.tensor_scalar, nc.vector.scalar_tensor_tensor, nc.vector.tensor_tensor
            steps = [0]

            def link(ins):
                steps[0] += 1
                ins.then_inc(dve_pro, 1)
                dve.wait_ge(dve_pro, steps[0])

            def power(L, src, j):
                bits = c1(L, TMP).bitcast(I32)
                link(ts(c1(L, TMP), src, 2.0 ** -20, None, ALU.max))
                link(ts(bits, bits, 0x7F800000, None, ALU.bitwise_and))
                link(ts(c1(L, S + j).bitcast(I32), bits, -1.0, float(268 << 23), ALU.mult, ALU.add))
                link(ts(c1(L, INV + j).bitcast(I32), bits, float(14 << 23), None, ALU.subtract))

            def split_weights(L, ms):
                g = cols[:, NV * L + G:NV * L + G + NC]
                for m in ms:
                    if L == 0:
                        dve.wait_ge(s_w0[m], 16)
                    else:
                        dve.wait_ge(s_stage[m % 2], 16 * (3 + m // 2))
                    link(nc.vector.tensor_reduce(kam[:, 0, :], wraw(L, m), AX.X, ALU.max, apply_absolute_value=True))
                    if m != WO:
                        link(tt(kam[:, 0, :], kam[:, 0, :], gabs[:, :], ALU.mult))
                    nc.vector.reduce_max(c1(L, AM + m), kam[:, 0, :], AX.X).then_inc(dve_am, 1)
                    dve.wait_ge(pool_am, 5 * L + m + 1)
                    power(L, c1(L, AR + m), m)
                    if m != WO:
                        ins = ts(gs[:, m, :], g, c1(L, S + m), None, ALU.mult)
                    else:
                        ins = ts(gs[:, m, :], ident[:, 0:NC], 0.0, c1(L, S + m), ALU.mult, ALU.add)
                    ins.then_inc(dve_scale, 1)
                    dve.wait_ge(dve_scale, 4 * L + m + 1)
                    dve.wait_ge(act_whi, 4 * L + m + 1)
                    for k in range(NC):
                        ins = stt(wsp[L][:, m, LO, k, :], wraw(L, m)[:, k, :], gs[:, m, k:k + 1], wsp[L][:, m, HI, k, :],
                                  ALU.mult, ALU.subtract)
                    ins.then_inc(dve_wlo, 1)
                    if m == WK:
                        dve.wait_ge(pe_bias, 3 * L + 1)
                        link(tt(bkp[:, L, :], ps[:, TAIL, 0:NC], cols[:, NV * L + BK:NV * L + BK + NC], ALU.add))
                        link(ts(c1(L, CK), c1(L, INV + WK), 1.0 / XS, None, ALU.mult))
                    elif m == WQ:
                        dve.wait_ge(pe_bias, 3 * L + 2)
                        dve.wait_ge(s_bc, 16 * 6)
                        link(tt(bc[L][:, 0, :], ps[:, TAIL + 1, :], bc[L][:, 0, :], ALU.add))
                        link(ts(c1(L, CQ), c1(L, INV + WQ), 1.0 / XS, None, ALU.mult))
                    elif m == WV:
                        dve.wait_ge(pe_bias, 3 * L + 3)
                        link(tt(bc[L][:, 1, :], ps[:, TAIL + 2, :], bc[L][:, 1, :], ALU.add))
                        link(ts(c1(L, CV), c1(L, INV + WV), 1.0 / XS, None, ALU.mult))
                        link(nc.vector.tensor_reduce(c1(L, TMP + 1), bc[L][:, 1, :], AX.X, ALU.max, apply_absolute_value=True))
                        link(stt(c1(L, TMP + 1), c1(L, AR + WV), float(D), c1(L, TMP + 1), ALU.mult, ALU.add))
                        power(L, c1(L, TMP + 1), VAL)
                        link(ts(c1(L, TMP + 2), c1(L, S + VAL), PS, None, ALU.mult))
                        link(tt(c1(L, TMP + 2), c1(L, TMP + 2), c1(L, TMP + 2), ALU.mult))
                        link(ts(c1(L, EPSY), c1(L, TMP + 2), EPS, None, ALU.mult))
                        link(ts(tab[L][:, :, 0:NT], tab[L][:, :, 0:NT], c1(L, S + VAL), None, ALU.mult))
                        nc.vector.tensor_copy(c1(L, TMP + 3), c1(L, EPSY)).then_inc(dve_prep, 1)

            def film(L):
                c0 = NV * L
                dve.wait_ge(pe_film, 4 * (L + 1))
                f = ps[:, TAIL, 0:NE * B].rearrange("p (c b) -> p c b", c=NE)
                for c in range(NC):
                    nc.vector.tensor_scalar(film_t[:, 0, c, :], f[:, c, :], cols[:, c0 + BE + c:c0 + BE + c + 1], 1.0, ALU.add, ALU.add)
                    ins = ts(film_t[:, 1, c, :], f[:, NC + c, :], cols[:, c0 + BE + NC + c:c0 + BE + NC + c + 1], None, ALU.add)
                link(ins)
                for c in range(NC):
                    ts(tab[L][:, :, 4 + c], film_t[:, 0, c, :], cols[:, c0 + FS + c:c0 + FS + c + 1], 0.5, ALU.mult, ALU.mult)
                    ins = stt(film_t[:, 1, c, :], film_t[:, 0, c, :], cols[:, c0 + FB + c:c0 + FB + c + 1], film_t[:, 1, c, :], ALU.mult, ALU.add)
                link(ins)
                for c in range(NC):
                    ins = ts(tab[L][:, :, 8 + c], film_t[:, 1, c, :], 0.5, None, ALU.mult)
                link(ins)
                a, b = film_t[:, 0, :, :].rearrange("p c b -> p b c"), film_t[:, 1, :, :].rearrange("p c b -> p b c")
                gain, shift = tab[L][:, :, 4:8], tab[L][:, :, 8:12]
                link(stt(a, gain, -1.0, gain, ALU.mult, ALU.max))
                link(stt(b, shift, -1.0, shift, ALU.mult, ALU.max))
                link(ts(film_t[:, 1, :, :], film_t[:, 1, :, :], 2.0, None, ALU.mult))
                link(stt(film_t[:, 0, :, :], film_t[:, 0, :, :], 2.0 * ROOT, film_t[:, 1, :, :], ALU.mult, ALU.add))
                nc.vector.reduce_max(c1(L, AM + FILM), film_t[:, 0, :, :].rearrange("p c b -> p (c b)"), AX.X).then_inc(dve_am, 1)
                dve.wait_ge(pool_am, 5 * L + 5)
                power(L, c1(L, AR + FILM), FILM)
                link(ts(tab[L][:, :, 4:12], tab[L][:, :, 4:12], c1(L, S + FILM), None, ALU.mult))
                tt(c1(L, CO), c1(L, INV + WO), c1(L, INV + FILM), ALU.mult).then_inc(dve_film, 1)
                dve.wait_ge(dve_film, L + 1)

            def x_stats(u, L, b, t, tails):
                if t == 0:
                    if L == 0:
                        dve.wait_ge(s_x, 16 * (b + 1))
                    else:
                        dve.wait_ge(dve_o, 4 * tails)
                nc.vector.bn_stats(xbs[:, t, :], xin[L][:, t, :]).then_inc(dve_xst, 1)

            def x_mean(u):
                for t in range(NT):
                    nc.vector.bn_aggr(xmv[:, t, :], xbs[:, t, :]).then_inc(dve_xag, 1)
                dve.wait_ge(dve_xag, 4 * u + 4)
                ts(xvar[:, :], xmv[:, :, 1], EPS, XS ** -2, ALU.add, ALU.mult).then_inc(dve_xvar, 1)

            def x_norm(u, L, t):
                if t == 0:
                    dve.wait_ge(pool_xstd, u + 1)
                    if reused(u, 1):
                        dve.wait_ge(pe_xt, 4 * u)
                ts(xh[:, t, :], xin[L][:, t, :], xmv[:, t, 0:1], xr_std[:, t:t + 1], ALU.subtract, ALU.mult).then_inc(dve_xh, 1)

            def x_lo(u, j):
                dve.wait_ge(act_xhi, 4 * u + j + 1)
                stt(xT[:, LO, j, :], ps[:, TR + j % 2, :], 1.0, xT[:, HI, j, :], ALU.mult, ALU.subtract).then_inc(dve_xlo, 1)

            def all_masked(u, b):
                dve.wait_ge(pool_madd, u + 1)
                nc.vector.reduce_max(nan0[:, 0:1], madd[:, :], AX.X).then_inc(dve_kb1, 1)
                dve.wait_ge(dve_kb1, 2 * b + 1)
                ts(nan0[:, 1:2], nan0[:, 0:1], 10.0, 0.0, ALU.mult, ALU.mult).then_inc(dve_kb1, 1)
                dve.wait_ge(dve_kb1, 2 * b + 2)
                ts(kbias[:, :], bkp[:, 0, :], nan0[:, 1:2], None, ALU.add).then_inc(dve_kb, 1)

            def step(u, A, Bu, N, between=None):
                v = u - 1

                def key_max(c, stats=False):
                    dve.wait_ge(pool_km, 4 * u + c + 1)
                    if stats:
                        dve.wait_ge(dve_xst, 4 * u + 8)
                    nc.vector.reduce_max(nkmax[:, c:c + 1], kf[:, c, :], AX.X, negate=True).then_inc(dve_kmax, 1)

                def y_stats(t):
                    dve.wait_ge(pe_y, 4 * v + t + 1)
                    nc.vector.bn_stats(ybs[:, t, :], ps[:, TAIL + (1 + t) % 3, :]).then_inc(dve_yst, 1)
                    n = count(dve, 4 * v + t + 1)
                    dve.wait_ge(s_rows, 16 * 12)
                    dve.wait_ge(dve_yst, n)
                    nc.vector.bn_aggr(ymv[:, t, :], ybs[:, t, :]).then_inc(dve_yag, 1)
                    dve.wait_ge(dve_yag, 4 * v + t + 1)
                    ts(yvar[:, t:t + 1], ymv[:, t, 1:2], c1(Bu[0], EPSY), None, ALU.add).then_inc(dve_yvar, 1)

                def y_shift(t):
                    dve.wait_ge(pool_ystd, 4 * v + t + 1)
                    stt(ynb[:, t:t + 1], ymv[:, t, 0:1], -1.0, yr_std[:, t:t + 1], ALU.mult, ALU.mult).then_inc(dve_ynb, 1)

                def query(t):
                    dve.wait_ge(pe_q, 4 * u + t + 1)
                    if t == 0 and Bu:
                        dve.wait_ge(pe_qt, 4 * u)
                    stt(qf[:, t, :], ps[:, PROJ + (4 + t) % 3, :], c1(A[0], CQ), bc[A[0]][:, 0, :], ALU.mult, ALU.add).then_inc(dve_q, 1)
                    dve.wait_ge(dve_q, 4 * u + t + 1)
                    nc.vector.reduce_max(nqmax[:, t, 0:HEADS[A[0]]], heads(qf[:, t, :], A[0]), AX.X, negate=True).then_inc(dve_qmax, 1)

                def query_sum(t):
                    dve.wait_ge(act_qe, 4 * u + t + 1)
                    h = HEADS[A[0]]
                    nc.vector.reduce_sum(qsum[:, t, 0:h], heads(qf[:, t, :], A[0]), AX.X).then_inc(dve_qs, 1)
                    dve.wait_ge(dve_qs, 4 * u + t + 1)
                    nc.vector.reciprocal(rq[:, t, 0:h], qsum[:, t, 0:h]).then_inc(dve_rq, 1)

                def silu(c):
                    dve.wait_ge(act_th, 4 * v + c + 1)
                    stt(z[:, c % 3, :], th[:, c % 2, :], 1.0, z[:, c % 3, :], ALU.add, ALU.mult).then_inc(dve_h, 1)

                def value(t):
                    dve.wait_ge(pe_v, 4 * u + t + 1)
                    if t >= 2 or Bu:
                        dve.wait_ge(dve_vlo, 4 * u + t - 1)
                    stt(vtmp[:, t % 2, :], ps[:, PROJ + (8 + t) % 3, :], c1(A[0], CV), bc[A[0]][:, 1, :], ALU.mult, ALU.add).then_inc(dve_v, 1)

                def v_lo(t):
                    dve.wait_ge(act_vhi, 4 * u + t + 1)
                    stt(Vs[:, LO, t, :], vtmp[:, t % 2, :], vms[:, t:t + 1], Vs[:, HI, t, :], ALU.mult, ALU.subtract).then_inc(dve_vlo, 1)

                def k_lo(t):
                    dve.wait_ge(act_khi, 4 * u + t + 1)
                    stt(Ks[:, LO, t, :], ps[:, TR + t % 2, :], 1.0, Ks[:, HI, t, :], ALU.mult, ALU.subtract).then_inc(dve_klo, 1)

                def q_lo(c):
                    dve.wait_ge(act_qhi, 4 * u + c + 1)
                    stt(qT[:, LO, c, :], ps[:, TR + c % 2, :], PS, qT[:, HI, c, :], ALU.mult, ALU.subtract).then_inc(dve_qlo, 1)

                def output(t):
                    dve.wait_ge(pe_o, 4 * v + t + 1)
                    L, b = Bu
                    if t == 0:
                        dve.wait_ge(pool_xr, 4 * u + 4 if L == 0 and A and A[0] == 1 else 4 * v + 4)
                        if L == 0 and isinstance(u, int) and u == 1:
                            dve.wait_ge(pe_film, 8)
                    dst = xin[1] if L == 0 else xr[1]
                    stt(dst[:, t, :], ps[:, TAIL + (5 + t) % 3, :], c1(L, CO), xr[L][:, t, :], ALU.mult, ALU.add).then_inc(dve_o, 1)

                if A:
                    key_max(0)
                if Bu:
                    dve.wait_ge(pe_at, v + 1)
                    if reused(u, 2):
                        dve.wait_ge(dve_alo, v)
                    stt(af[:, :], ps[:, TAIL, :], 1.0 / PS, diag[Bu[0]][:, :], ALU.mult, ALU.mult).then_inc(dve_af, 1)
                    dve.wait_ge(act_ahi, v + 1)
                    tt(As[:, LO, :], af[:, :], As[:, HI, :], ALU.subtract).then_inc(dve_alo, 1)
                if N:
                    x_stats(u + 1, *N, 0, v)
                if Bu:
                    y_stats(0)
                if A:
                    if N:
                        x_stats(u + 1, *N, 1, v)
                    key_max(1)
                if Bu:
                    y_shift(0)
                if N:
                    x_stats(u + 1, *N, 2, v)
                    x_stats(u + 1, *N, 3, v)
                if Bu:
                    y_stats(1)
                if A:
                    key_max(2, stats=bool(N))
                if N:
                    x_mean(u + 1)
                if Bu:
                    y_shift(1)
                    y_stats(2)
                if A:
                    key_max(3)
                if Bu:
                    y_shift(2)
                if A:
                    query(0)
                if Bu:
                    y_stats(3)
                if A:
                    dve.wait_ge(act_ke, 4 * u + 4)
                    nc.vector.reciprocal(rk[:, :], ksum[:, :]).then_inc(dve_ksum, 1)
                if Bu:
                    y_shift(3)
                if A:
                    query(1)
                    query_sum(0)
                    query(2)
                    query_sum(1)
                    query(3)
                if A:
                    query_sum(2)
                if Bu:
                    silu(0)
                    silu(1)
                if A:
                    query_sum(3)
                    value(0)
                if A:
                    v_lo(0)
                    value(1)
                    k_lo(0)
                    k_lo(1)
                    v_lo(1)
                if Bu:
                    silu(2)
                    silu(3)
                if A:
                    value(2)
                    k_lo(2)
                    k_lo(3)
                    v_lo(2)
                    value(3)
                    q_lo(0)
                    q_lo(1)
                    v_lo(3)
                if N:
                    for t in range(NT):
                        x_norm(u + 1, N[0], t)
                if between:
                    between()
                if Bu:
                    output(0)
                if A:
                    q_lo(2)
                    q_lo(3)
                if Bu:
                    output(1)
                if N:
                    x_lo(u + 1, 0)
                    x_lo(u + 1, 1)
                if Bu:
                    output(2)
                if N:
                    if N[0] == 0:
                        all_masked(u + 1, N[1])
                    x_lo(u + 1, 2)
                    x_lo(u + 1, 3)
                if Bu:
                    output(3)

            def prepare(u, L, b):
                for t in range(NT):
                    x_stats(u, L, b, t, u - 1)
                dve.wait_ge(dve_xst, 4 * u + 4)
                x_mean(u)
                for t in range(NT):
                    x_norm(u, L, t)
                for j in range(NC):
                    x_lo(u, j)

            dve.wait_ge(s_small, 48)
            link(ts(vtmp[0:B, 0, :], vtmp[0:B, 0, :].bitcast(I32), 1.0, -1.0, ALU.is_equal, ALU.mult))
            zc, tc = z[0:B, 0:2, :].rearrange("p a n -> p (a n)"), th[0:B, :, :].rearrange("p a n -> p (a n)")
            link(ts(zc, zc, 0.5, None, ALU.mult))
            link(ts(vtmp[0:B, 0, :], vtmp[0:B, 0, :], 1.0, None, ALU.add))
            dve.wait_ge(act_pro, 1)
            link(stt(zc, tc, 1.0, zc, ALU.add, ALU.mult))
            dve.wait_ge(pe_pro, 1)
            link(nc.vector.tensor_copy(cols[:, :], ps[:, TR, 0:2 * NV]))
            dve.wait_ge(pe_pro, 2)
            link(nc.vector.tensor_copy(embT[:, :, :], ps[:, TR + 1, 0:NE * B].rearrange("p (k b) -> p k b", k=NE)))
            for L in range(2):
                c = (NE + NT * L) * B
                link(nc.vector.tensor_copy(tab[L][:, :, 0:NT], ps[:, TR + 1, c:c + NT * B].rearrange("p (t b) -> p b t", t=NT)))

            def norm_vectors(L):
                g, b = (cols[:, NV * L + j:NV * L + j + NC] for j in (G, LNB))
                link(stt(gabs[:, :], g, -1.0, g, ALU.mult, ALU.max))
                link(nc.vector.tensor_copy(af[:, :].rearrange("p (k n) -> p k n", k=NC),
                                           b.rearrange("p (k n) -> p k n", n=1).to_broadcast((P, NC, P))))
                nc.vector.tensor_copy(c1(L, TMP + 4), gabs[:, 0:1]).then_inc(dve_bias, 1)

            def second_layer():
                norm_vectors(1)
                split_weights(1, (WK, WQ, WV, WO))
                film(1)

            norm_vectors(0)
            prepare(0, 0, 0)
            split_weights(0, (WK, WQ, WV))
            all_masked(0, 0)
            step(0, (0, 0), None, None)
            split_weights(0, (WO,))
            film(0)
            prepare(1, 0, 1)
            all_masked(1, 1)
            step(1, (0, 1), (0, 0), None, between=second_layer)
            prepare(2, 1, 0)
            with dve.Fori(1, B - 1) as i:
                step(2 * i, (1, i - 1), (0, i), (0, i + 1))
                step(2 * i + 1, (0, i + 1), (1, i - 1), (1, i))
            step(30, (1, 14), (0, 15), None)
            prepare(31, 1, 15)
            step(31, (1, 15), (1, 14), None)
            step(32, None, (1, 15), None)

        @block.tensor
        def _(pe):
            mm = nc.tensor.matmul

            def prepare(u):
                for j in range(NC):
                    x_transpose(u, j)

            def x_transpose(u, j):
                if j == 0:
                    pe.wait_ge(dve_xh, 4 * u + 4)
                if j >= 2:
                    pe.wait_ge(dve_xlo, 4 * u + j - 1)
                elif reused(u, 1):
                    pe.wait_ge(dve_qlo, 4 * u - 1 + j)
                for t in range(NT):
                    last = nc.tensor.transpose(ps[:, TR + j % 2, P * t:P * t + P], xh[:, t, P * j:P * j + P], ident[:, :])
                last.then_inc(pe_xt, 1)

            def bias(L):
                for m in (WK, WQ, WV):
                    if L == 0:
                        pe.wait_ge(s_w0[m], 16)
                    else:
                        pe.wait_ge(s_stage[m % 2], 16 * (3 + m // 2))
                    pe.wait_ge(dve_bias, L + 1)
                    W = wraw(L, m)
                    if m == WK:
                        for c in range(NC):
                            for k in range(NC):
                                last = mm(ps[:, TAIL, c:c + 1], W[:, k, P * c:P * c + P], af[:, P * k:P * k + 1],
                                          start=(k == 0), stop=(k == NC - 1))
                    else:
                        for k in range(NC):
                            last = mm(ps[:, TAIL + m, :], af[:, P * k:P * k + P], W[:, k, :], start=(k == 0), stop=(k == NC - 1))
                    last.then_inc(pe_bias, 1)

            def film(L):
                pe.wait_ge(dve_prep, L + 1)
                for q in range(4):
                    j = q + 8 * L
                    pe.wait_ge(s_stage[j % 2], 16 * (j // 2 + 1))
                    for c in (2 * q, 2 * q + 1):
                        for k in range(NE):
                            last = mm(ps[:, TAIL, B * c:B * c + B], quarter(j)[:, k, P * (c % 2):P * (c % 2) + P], embT[:, k, :],
                                      start=(k == 0), stop=(k == NE - 1))
                    last.then_inc(pe_film, 1)

            def step(u, A, Bu, N, between=None):
                v = u - 1

                def product(bank, stationary, moving):
                    n = 0
                    for a, b in PRODUCTS:
                        for k in range(NC):
                            last = mm(ps[:, bank, :], stationary(a, k), moving(b, k), start=(n == 0), stop=(n == 11))
                            n += 1
                    return last

                def keys(c):
                    if c == 0:
                        pe.wait_ge(dve_xlo, 4 * u + 4)
                        pe.wait_ge(dve_wlo, 4 * A[0] + 1)
                    if c < 3:
                        if Bu:
                            pe.wait_ge(dve_v, 4 * u - 2 + c)
                    else:
                        pe.wait_ge(act_kf, 4 * u + 1)
                    W = wsp[A[0]][:, WK]
                    product(PROJ + c % 3, lambda a, k: W[:, a, k, P * c:P * c + P], lambda b, k: xT[:, b, k, :]).then_inc(pe_k, 1)

                def queries(t):
                    if t < 3:
                        pe.wait_ge(act_kf, 4 * u + t + 2)
                    else:
                        pe.wait_ge(dve_q, 4 * u + 1)
                    if t == 0:
                        pe.wait_ge(dve_wlo, 4 * A[0] + 2)
                    W = wsp[A[0]][:, WQ]
                    product(PROJ + (4 + t) % 3, lambda a, k: xT[:, a, k, P * t:P * t + P], lambda b, k: W[:, b, k, :]).then_inc(pe_q, 1)

                def values(t):
                    if t < 3:
                        pe.wait_ge(dve_q, 4 * u + t + 2)
                    else:
                        pe.wait_ge(dve_v, 4 * u + 1)
                    if t == 0:
                        pe.wait_ge(dve_wlo, 4 * A[0] + 3)
                    W = wsp[A[0]][:, WV]
                    product(PROJ + (8 + t) % 3, lambda a, k: xT[:, a, k, P * t:P * t + P], lambda b, k: W[:, b, k, :]).then_inc(pe_v, 1)

                def attention():
                    pe.wait_ge(dve_vlo, 4 * v + 4)
                    pe.wait_ge(dve_klo, 4 * v + 4)
                    if reused(u, 2):
                        pe.wait_ge(dve_o, 4 * v - 2)
                    st, mv = (Vs, Ks) if Bu[0] == 0 else (Ks, Vs)
                    for c in range(NC):
                        n = 0
                        for a, b in PRODUCTS:
                            for t in range(NT):
                                last = mm(ps[:, TAIL, P * c:P * c + P], st[:, a, t, P * c:P * c + P], mv[:, b, t, P * c:P * c + P],
                                          start=(n == 0), stop=(n == 11))
                                n += 1
                    last.then_inc(pe_at, 1)

                def ys(t):
                    if t == 0:
                        pe.wait_ge(dve_qlo, 4 * v + 4)
                        pe.wait_ge(dve_alo, v + 1)
                    if t < 2:
                        if reused(u, 2):
                            pe.wait_ge(dve_o, 4 * v - 1 + t)
                    elif t == 3:
                        pe.wait_ge(act_yh, 4 * v + 1)
                    for c in range(NC):
                        for n, (a, b) in enumerate(PRODUCTS):
                            last = mm(ps[:, TAIL + (1 + t) % 3, P * c:P * c + P], qT[:, a, c, P * t:P * t + P], As[:, b, P * c:P * c + P],
                                      start=(n == 0), stop=(n == 2))
                    last.then_inc(pe_y, 1)

                def y_transpose(c):
                    if c == 0:
                        pe.wait_ge(act_yh, 4 * v + 4)
                    if c < 2:
                        if not A:
                            pe.wait_ge(dve_qlo, 4 * v + 3 + c)
                    else:
                        pe.wait_ge(act_z, 4 * v + c - 1)
                    for t in range(NT):
                        last = nc.tensor.transpose(ps[:, TR + c % 2, P * t:P * t + P], yh[:, t, P * c:P * c + P], ident[:, :])
                    last.then_inc(pe_yt, 1)

                def k_transpose(t):
                    if t == 0:
                        pe.wait_ge(pool_kn, 4 * u + 4)
                    if t >= 2:
                        pe.wait_ge(dve_klo, 4 * u + t - 1)
                    elif Bu:
                        pe.wait_ge(act_z, 4 * v + 3 + t)
                    for c in range(NC):
                        last = nc.tensor.transpose(ps[:, TR + t % 2, P * c:P * c + P], kf[:, c, P * t:P * t + P], ident[:, :])
                    last.then_inc(pe_kt, 1)

                def q_transpose(c):
                    if c == 0:
                        pe.wait_ge(pool_qn, 4 * u + 4)
                    if c >= 2:
                        pe.wait_ge(dve_qlo, 4 * u + c - 1)
                    else:
                        pe.wait_ge(dve_klo, 4 * u + 3 + c)
                    for t in range(NT):
                        last = nc.tensor.transpose(ps[:, TR + c % 2, P * t:P * t + P], qf[:, t, P * c:P * c + P], ident[:, :])
                    last.then_inc(pe_qt, 1)

                def output(t):
                    if t == 0:
                        pe.wait_ge(pool_hlo, 4 * v + 4)
                        pe.wait_ge(dve_wlo, 4 * Bu[0] + 4)
                    if t < 3:
                        pe.wait_ge(act_yh, 4 * v + t + 2)
                    else:
                        pe.wait_ge(dve_o, 4 * v + 1)
                    W = wsp[Bu[0]][:, WO]
                    product(TAIL + (5 + t) % 3, lambda a, k: hT[:, a, k, P * t:P * t + P], lambda b, k: W[:, b, k, :]).then_inc(pe_o, 1)

                if A:
                    keys(0)
                if Bu:
                    attention()
                if A:
                    keys(1)
                if Bu:
                    ys(0)
                if A:
                    keys(2)
                if Bu:
                    ys(1)
                if A:
                    keys(3)
                if Bu:
                    ys(2)
                if A:
                    queries(0)
                if Bu:
                    ys(3)
                if A:
                    queries(1)
                    queries(2)
                if Bu:
                    y_transpose(0)
                    y_transpose(1)
                if A:
                    queries(3)
                if Bu:
                    y_transpose(2)
                    y_transpose(3)
                if A:
                    values(0)
                    values(1)
                    k_transpose(0)
                    k_transpose(1)
                    values(2)
                    k_transpose(2)
                    k_transpose(3)
                    values(3)
                    q_transpose(0)
                    q_transpose(1)
                if between:
                    between()
                if Bu:
                    output(0)
                if A:
                    q_transpose(2)
                    q_transpose(3)
                if Bu:
                    output(1)
                if N:
                    x_transpose(u + 1, 0)
                    x_transpose(u + 1, 1)
                if Bu:
                    output(2)
                if N:
                    x_transpose(u + 1, 2)
                    x_transpose(u + 1, 3)
                if Bu:
                    output(3)

            pe.wait_ge(pool_const, 5)
            pe.wait_ge(s_rows, 16 * 12)
            nc.tensor.transpose(ps[:, TR, 0:2 * NV], rows[:, :], ident[0:2 * NV, 0:2 * NV]).then_inc(pe_pro, 1)
            pe.wait_ge(dve_pro, 4)
            for k in range(NE):
                nc.tensor.transpose(ps[:, TR + 1, B * k:B * k + B], z[0:B, k // 4, P * (k % 4):P * (k % 4) + P], ident[0:B, 0:B])
            for L in range(2):
                for t in range(NT):
                    c = (NE + NT * L + t) * B
                    last = nc.tensor.transpose(ps[:, TR + 1, c:c + B], vtmp[0:B, L, P * t:P * t + P], ident[0:B, 0:B])
            last.then_inc(pe_pro, 1)
            pe.wait_ge(dve_pro, 8)
            prepare(0)
            bias(0)
            step(0, (0, 0), None, None)
            film(0)
            prepare(1)
            pe.wait_ge(dve_film, 1)

            def second_layer():
                pe.wait_ge(act_yh, 4)
                bias(1)
                film(1)
                pe.wait_ge(dve_film, 2)

            step(1, (0, 1), (0, 0), None, between=second_layer)
            prepare(2)
            with pe.Fori(1, B - 1) as i:
                step(2 * i, (1, i - 1), (0, i), (0, i + 1))
                step(2 * i + 1, (0, i + 1), (1, i - 1), (1, i))
            step(30, (1, 14), (0, 15), None)
            prepare(31)
            step(31, (1, 15), (1, 14), None)
            step(32, None, (1, 15), None)


_W = [[f"L0_cond_{n}" for n in ("Wk", "Wq", "Wv", "film_out_W", "film_emb_W")],
      [f"L1_cond_{n}" for n in ("Wk", "Wq", "Wv", "W_out", "W_emb")]]
_VEC = [dict(g="norm_scale", lnb="norm_bias", fs="film_norm_scale", fb="film_norm_bias", bk="bk", be="film_emb_b", bq="bq", bv="bv",
             bo="film_out_b"),
        dict(g="ln_w", lnb="ln_b", fs="ln2_w", fb="ln2_b", bk="bk", be="b_emb", bq="bq", bv="bv", bo="b_out")]


def kernel(**inputs):
    import numpy as _np
    import concourse.bacc as _bacc
    from concourse import mybir as _mybir
    from concourse.bass_utils import run_bass_kernel_spmd as _run

    nc = _bacc.Bacc("TRN2", target_bir_lowering=False, num_devices=1)
    arrays = {}

    def dram(name, shape=None):
        a = _np.ascontiguousarray(inputs[name])
        if shape:
            a = a.reshape(shape)
        arrays[f"in_{name}"] = a
        return nc.dram_tensor(f"in_{name}", a.shape, _mybir.dt.from_np(a.dtype), kind="ExternalInput").ap()

    x, cond = dram("x"), dram("cond_2048")
    mask0, mask1 = dram("mask_BxS_ik0"), dram("mask_BxSx1_fk1", (B, T))
    w = [[dram(n) for n in names] for names in _W]
    vec = [{k: dram(f"L{L}_cond_{n}") for k, n in names.items()} for L, names in enumerate(_VEC)]
    out = nc.dram_tensor("out_0", (B, T, D), F32, kind="ExternalOutput").ap()
    build(nc, x, cond, mask0, mask1, w, vec, out)
    r = _run(nc, [arrays], core_ids=[0])
    return r.results[0]["out_0"]
```

```python
from contextlib import ExitStack

import concourse.bass as bass
from concourse import mybir

F32, F16, BF16, I32 = mybir.dt.float32, mybir.dt.float16, mybir.dt.bfloat16, mybir.dt.int32
ALU = mybir.AluOpType
ACT = mybir.ActivationFunctionType
AX = mybir.AxisListType

P = 128
B, T, D, E = 16, 512, 512, 1024
NT, NC, NE = T // P, D // P, E // P
HEADS = (16, 8)
EPS = 1e-5
XS = 2048.0
PS = 16384.0
ROOT = 22.63
MASKED = -3.0e38
WK, WQ, WV, WO = range(4)
HI, LO = 0, 1
G, LNB, FS, FB, BK, BE = 0, 4, 8, 12, 16, 20
NV = 28
PRODUCTS = ((HI, HI), (HI, LO), (LO, HI))
LAST = (0, 1, 2, 7)
PROJ, TR, TAIL = 0, 3, 5


def build(nc, x, cond, mask0, mask1, w, vec, out):
    with ExitStack() as ctx:
        def sb(name, shape, dt):
            return ctx.enter_context(nc.sbuf_tensor(name, shape, dt))

        def sem(name):
            return ctx.enter_context(nc.semaphore(name))

        wsp = [sb(f"wsp{L}", [P, 4, 2, NC, D], F16) for L in range(2)]
        xin = [sb(f"xin{L}", [P, NT, D], F32) for L in range(2)]
        xr = [sb(f"xr{L}", [P, NT, D], F32) for L in range(2)]
        xh = sb("xh", [P, NT, D], F32)
        yh = sb("yh", [P, NT, D], F32)
        xT = sb("xT", [P, 2, NC, T], F16)
        kf = sb("kf", [P, NC, T], F32)
        qf = sb("qf", [P, NT, D], F32)
        Ks = sb("Ks", [P, 2, NT, D], F16)
        Vs = sb("Vs", [P, 2, NT, D], F16)
        qT = sb("qT", [P, 2, NC, T], F16)
        hT = sb("hT", [P, 2, NC, T], F16)
        af = sb("af", [P, D], F32)
        As = sb("As", [P, 2, D], F16)
        vtmp = sb("vtmp", [P, 2, D], F32)
        z = sb("z", [P, 3, T], F32)
        th = sb("th", [P, 2, T], F32)
        madd = sb("madd", [P, T], F32)
        bc = [sb(f"bc{L}", [P, 3, D], F32) for L in range(2)]
        diag = [sb(f"diag{L}", [P, D], BF16) for L in range(2)]
        ident = sb("ident", [P, P], F32)
        rows = sb("rows", [2 * NV, P], F32)
        cols = sb("cols", [P, 2 * NV], F32)
        embT = sb("embT", [P, NE, B], F32)
        tab = [sb(f"tab{L}", [P, B, 12], F32) for L in range(2)]
        film_t = sb("film_t", [P, 2, NC, B], F32)
        vms = sb("vms", [P, NT], F32)
        ghs = sb("ghs", [P, 8], F32)
        sc = [sb(f"sc{L}", [P, 40], F32) for L in range(2)]
        gs = sb("gs", [P, 4, NC], F32)
        gabs = sb("gabs", [P, NC], F32)
        kam = sb("kam", [P, 2, NC], F32)
        bkp = sb("bkp", [P, 2, NC], F32)
        kbias = sb("kbias", [P, NC], F32)
        nan0 = sb("nan0", [P, 2], F32)
        nkmax = sb("nkmax", [P, NC], F32)
        ksum = sb("ksum", [P, NC], F32)
        rk = sb("rk", [P, NC], F32)
        nqmax = sb("nqmax", [P, NT, 16], F32)
        qsum = sb("qsum", [P, NT, 16], F32)
        rq = sb("rq", [P, NT, 16], F32)
        xbs = sb("xbs", [P, NT, 6], F32)
        xmv = sb("xmv", [P, NT, 2], F32)
        xvar = sb("xvar", [P, NT], F32)
        xr_std = sb("xr_std", [P, NT], F32)
        ybs = sb("ybs", [P, NT, 6], F32)
        ymv = sb("ymv", [P, NT, 2], F32)
        yvar = sb("yvar", [P, NT], F32)
        yr_std = sb("yr_std", [P, NT], F32)
        ynb = sb("ynb", [P, NT], F32)
        mhalf = sb("mhalf", [P, NT], F32)
        ps = ctx.enter_context(nc.psum_tensor("ps", [P, 8, 512], F32))

        AM, AR, S, INV = 0, 6, 12, 18
        CK, CQ, CV, CO, EPSY = 24, 25, 26, 27, 28
        TMP = 30
        FILM, VAL = 4, 5

        def raw(m):
            return wsp[1][:, m].rearrange("p a k n -> p (a k n)").bitcast(F32).rearrange("p (k n) -> p k n", k=NC)

        stage = (xr[1][:, :, :], xin[1][:, :, :], yh[:, :, :],
                 hT[:, :, :, :].rearrange("p a k n -> p (a k n)").bitcast(F32).rearrange("p (k n) -> p k n", k=NC), xh[:, :, :])
        FILM_STAGE = ((0, 1, 2, 3), (0, 1, 0, 2))
        FILM_LOAD = ((1, 1, 1, 1), (3, 3, 4, 3))
        WEIGHT_STAGE, WEIGHT_LOAD = (0, 1, 2, 4), (2, 2, 2, 1)

        def wraw(L, m):
            return raw(m) if L == 0 else stage[WEIGHT_STAGE[m]]

        def quarter(L, q):
            return stage[FILM_STAGE[L][q]].rearrange("p t n -> p (t n)").rearrange("p (k n) -> p k n", k=NE)

        s_x, s_rows, s_bc, s_small, s_mask = sem("s_x"), sem("s_rows"), sem("s_bc"), sem("s_small"), sem("s_mask")
        s_w0 = [sem(f"s_w0_{m}") for m in range(4)]
        s_stage = [sem(f"s_stage{i}") for i in range(5)]
        s_store = [sem(f"s_store{t}") for t in range(NT)]
        pool_const, dve_pro, act_pro, pe_pro = sem("pool_const"), sem("dve_pro"), sem("act_pro"), sem("pe_pro")
        pe_bias, pe_film, act_whi, dve_wlo, pool_part, pool_wlo, dve_film = (
            sem(n) for n in ("pe_bias", "pe_film", "act_whi", "dve_wlo", "pool_part", "pool_wlo", "dve_film"))
        dve_filmam, pool_filmam, dve_biasq = sem("dve_filmam"), sem("pool_filmam"), sem("dve_biasq")
        dve_am, pool_am, dve_scale, dve_bias = sem("dve_am"), sem("pool_am"), sem("dve_scale"), sem("dve_bias")
        dve_keys, dve_emb, dve_fcopy, act_fcopy, pe_ft = (sem(n) for n in ("dve_keys", "dve_emb", "dve_fcopy", "act_fcopy", "pe_ft"))
        dve_prep = sem("dve_prep")
        pe_xt, pe_k, pe_q, pe_v, pe_kt, pe_qt = (sem(f"pe_{n}") for n in ("xt", "k", "q", "v", "kt", "qt"))
        pe_at, pe_y, pe_yt, pe_o = (sem(f"pe_{n}") for n in ("at", "y", "yt", "o"))
        act_xhi, act_kf, act_ke, act_khi, act_qe, act_qhi, act_vhi = (sem(f"act_{n}") for n in ("xhi", "kf", "ke", "khi", "qe", "qhi", "vhi"))
        act_ahi, act_yh, act_z, act_th, act_hhi = (sem(f"act_{n}") for n in ("ahi", "yh", "z", "th", "hhi"))
        dve_xst, dve_xag, dve_xvar, dve_xh, dve_xlo = (sem(f"dve_{n}") for n in ("xst", "xag", "xvar", "xh", "xlo"))
        dve_kmax, dve_ksum, dve_klo, dve_kb, dve_kb1 = (sem(f"dve_{n}") for n in ("kmax", "ksum", "klo", "kb", "kb1"))
        dve_q, dve_qmax, dve_qs, dve_rq, dve_qlo = (sem(f"dve_{n}") for n in ("q", "qmax", "qs", "rq", "qlo"))
        dve_v, dve_vlo, dve_af, dve_alo = (sem(f"dve_{n}") for n in ("v", "vlo", "af", "alo"))
        dve_yst, dve_yag, dve_yvar, dve_ynb = (sem(f"dve_{n}") for n in ("yst", "yag", "yvar", "ynb"))
        dve_h, dve_o = sem("dve_h"), sem("dve_o")
        pool_vm, pool_gh, pool_km, pool_kn, pool_qs, pool_qn, pool_xr, pool_xstd, pool_ystd, pool_madd, pool_hlo = (
            sem(f"pool_{n}") for n in ("vm", "gh", "km", "kn", "qs", "qn", "xr", "xstd", "ystd", "madd", "hlo"))

        def c1(L, j):
            return sc[L][:, j:j + 1]

        def film_place(buf, q, n):
            return buf[0:B, q // 2, 256 * (q % 2):256 * (q % 2) + n]

        def zc(c):
            return z[:, c, :] if c < 3 else af[:, :]

        def heads(ap, L):
            return ap.rearrange("p (h e) -> p h e", h=HEADS[L])

        def per_head(ap, L):
            return ap[:, 0:HEADS[L]].rearrange("p (h e) -> p h e", e=1).to_broadcast((P, HEADS[L], D // HEADS[L]))

        x_rows = x.rearrange("b (t p) d -> b p t d", p=P)
        out_rows = out.rearrange("b (t p) d -> b p t d", p=P)

        def wait_split(eng, L, m):
            if 4 * L + m < 3:
                eng.wait_ge(dve_wlo, m + 1)
            else:
                eng.wait_ge(pool_wlo, 4 * L + m - 2)

        def reused(u, n):
            return not (isinstance(u, int) and u < n)

        def count(eng, n):
            return n if isinstance(n, int) else eng.snap(eng.to_reg(n))

        block = ctx.enter_context(nc.Block())

        @block.sync
        def _(sp):
            for t in range(NT):
                sp.sem_inc(s_store[t], 16)
            sp.dma_start(xin[0][:, :, :], x_rows[0]).then_inc(s_x, 16)
            for L in range(2):
                r = NV * L
                for name, n in (("g", 4), ("lnb", 4), ("fs", 4), ("fb", 4), ("bk", 4), ("be", 8)):
                    sp.dma_start(rows[r:r + n, :], vec[L][name].rearrange("(r p) -> r p", p=P)).then_inc(s_rows, 16)
                    r += n
            for m in (WK, WQ, WV):
                sp.dma_start(raw(m), w[0][m].rearrange("(k p) n -> p k n", p=P)).then_inc(s_w0[m], 16)
                if m == WK:
                    sp.dma_start(vtmp[0:B, 0, :].bitcast(I32), mask0).then_inc(s_small, 16)
                    sp.dma_start(vtmp[0:B, 1, :], mask1).then_inc(s_small, 16)
                    sp.dma_start(z[0:B, 0:2, :].rearrange("p a n -> p (a n)"), cond).then_inc(s_small, 16)
                    sp.dma_start(madd[:, :].bitcast(I32), mask0[0:1, :].to_broadcast((P, T))).then_inc(s_mask, 16)
                if m == WQ:
                    for L in range(2):
                        for j, name in enumerate(("bq", "bv", "bo")):
                            sp.dma_start(bc[L][:, j, :], vec[L][name].rearrange("(a n) -> a n", a=1).to_broadcast((P, D))).then_inc(s_bc, 16)

            def load_mask(u, L, b, tests):
                n0 = count(sp, 4 * u)
                n1 = count(sp, tests)
                sp.wait_ge(s_rows, 16 * 12)
                sp.wait_ge(pool_km, n0)
                sp.wait_ge(dve_kb, n1)
                if L == 1:
                    sp.dma_start(madd[:, :], mask1[bass.ds(b, 1), :].to_broadcast((P, T))).then_inc(s_mask, 16)
                else:
                    sp.dma_start(madd[:, :].bitcast(I32), mask0[bass.ds(b, 1), :].to_broadcast((P, T))).then_inc(s_mask, 16)

            def load_x(b, before):
                n0 = count(sp, 4 * before + 4)
                n1 = count(sp, 4 * before + 4)
                sp.wait_ge(s_rows, 16 * 12)
                sp.wait_ge(dve_xh, n0)
                sp.wait_ge(pool_xr, n1)
                sp.dma_start(xin[0][:, :, :], x_rows[b]).then_inc(s_x, 16)

            def load_weight(m):
                if m == WO:
                    sp.wait_ge(pe_xt, 8)
                else:
                    sp.wait_ge(pe_film, m + 1)
                sp.dma_start(wraw(1, m), w[1][m].rearrange("(k p) n -> p k n", p=P)).then_inc(s_stage[WEIGHT_STAGE[m]], 16)

            def load_film(L, q):
                i = FILM_STAGE[L][q]
                if L == 1 and q == 2:
                    sp.wait_ge(pe_film, 6)
                elif L == 1:
                    sp.wait_ge(act_whi, 4 + i + 1)
                    wait_split(sp, 1, i)
                    sp.wait_ge(pe_bias, 3 + i + 1)
                sp.dma_start(stage[i].rearrange("p t n -> p (t n)").rearrange("p (k n) -> p k n", k=NE),
                             w[L][4].rearrange("(k p) n -> p k n", p=P)[:, :, 256 * q:256 * q + 256]).then_inc(s_stage[i], 16)

            for q in range(4):
                load_film(0, q)
            sp.dma_start(raw(WO), w[0][WO].rearrange("(k p) n -> p k n", p=P)).then_inc(s_w0[WO], 16)
            load_x(1, 0)
            load_mask(1, 0, 1, 1)
            for m in (WK, WQ, WV):
                load_weight(m)
            load_film(1, 0)
            load_weight(WO)
            load_film(1, 1)
            load_mask(2, 1, 0, 2)
            sp.wait_ge(pe_yt, 4)
            load_film(1, 3)
            load_film(1, 2)

            def store(b, u):
                for t in range(NT):
                    n = count(sp, 4 * u + t + 1)
                    sp.wait_ge(s_rows, 16 * 12)
                    sp.wait_ge(dve_o, n)
                    sp.dma_start(out_rows[b][:, t, :], xr[1][:, t, :]).then_inc(s_store[t], 16)

            with sp.Fori(1, B - 1) as i:
                load_x(i + 1, 2 * i - 1)
                load_mask(2 * i + 1, 0, i + 1, i + 1)
                load_mask(2 * i + 2, 1, i, i + 2)
                store(i - 1, 2 * i)
            load_mask(31, 1, 15, 16)
            store(14, 30)
            store(15, 31)
            for t in range(NT):
                sp.wait_ge(s_store[t], 16 * (B + 1))

        @block.gpsimd
        def _(pool):
            def tt(o, a, b, op):
                return nc.gpsimd.tensor_tensor(o, a, b, op)

            pool.memset(ident[:, :], 0.0).then_inc(pool_const, 1)
            pool.memset(mhalf[:, :], -0.5).then_inc(pool_const, 1)
            for L in range(2):
                pool.memset(diag[L][:, :], 1.0).then_inc(pool_const, 1)
            pool.wait_ge(pool_const, 4)
            pool.affine_select(out=ident[:, :], in_=ident[:, :], compare_op=ALU.not_equal, fill=1.0, base=0,
                               pattern=[[-1, P]], channel_multiplier=1).then_inc(pool_const, 1)
            n = 5
            for L in range(2):
                hd = D // HEADS[L]
                v = diag[L][:, :].rearrange("p (c h e) -> p c h e", c=NC, e=hd)
                pool.affine_select(out=v, in_=v, compare_op=ALU.is_ge, fill=0.0, base=0,
                                   pattern=[[0, NC], [-hd, P // hd], [0, hd]], channel_multiplier=1).then_inc(pool_const, 1)
                n += 1
                pool.wait_ge(pool_const, n)
                pool.affine_select(out=v, in_=v, compare_op=ALU.is_ge, fill=0.0, base=hd - 1,
                                   pattern=[[0, NC], [hd, P // hd], [0, hd]], channel_multiplier=-1).then_inc(pool_const, 1)
                n += 1

            def bound(L, j):
                have, done, n = (dve_am, pool_am, 4 * L + j + 1) if j < FILM else (dve_filmam, pool_filmam, L + 1)
                pool.wait_ge(have, n)
                pool.partition_all_reduce(c1(L, AR + j), c1(L, AM + j), P, bass.bass_isa.ReduceOp.max).then_inc(done, 1)

            def weight_lo(L, m):
                pool.wait_ge(act_whi, 4 * L + m + 1)
                for k in range(NC):
                    i = 4 * (4 * L + m - 3) + k
                    if i >= 2:
                        pool.wait_ge(pool_part, 2 * i - 2)
                    else:
                        pool.wait_ge(dve_emb, 1)
                    pool.tensor_scalar(th[:, k % 2, :], wraw(L, m)[:, k, :], gs[:, m, k:k + 1], 1.0, ALU.mult, ALU.mult).then_inc(pool_part, 1)
                    pool.wait_ge(pool_part, 2 * i + 1)
                    tt(wsp[L][:, m, LO, k, :], th[:, k % 2, :], wsp[L][:, m, HI, k, :], ALU.subtract).then_inc(pool_part, 1)
                pool.wait_ge(pool_part, 2 * i + 2)
                pool.sem_inc(pool_wlo, 1)

            def mask_add(u, L):
                n = count(pool, 16 * (u + 1))
                pool.wait_ge(pool_const, 4)
                pool.wait_ge(s_mask, n)
                if L == 0:
                    pool.tensor_scalar(madd[:, :], madd[:, :].bitcast(I32), 1.0, MASKED, ALU.is_equal, ALU.mult).then_inc(pool_madd, 1)
                else:
                    pool.tensor_scalar(madd[:, :], madd[:, :], 1.0, 1.0e6, ALU.subtract, ALU.mult).then_inc(pool_madd, 1)

            def x_std(u):
                pool.wait_ge(dve_xvar, u + 1)
                tt(xr_std[:, :], xvar[:, :], mhalf[:, :], ALU.pow).then_inc(pool_xstd, 1)

            def prepare(u, L, b):
                x_std(u)
                mask_add(u, L)

            def residual(u, L, b, t):
                if L == 1:
                    pool.wait_ge(s_store[t], 16 * (b + 1))
                tt(xr[L][:, t, :], xin[L][:, t, :], bc[L][:, 2, :], ALU.add).then_inc(pool_xr, 1)

            def step(u, A, Bu, N, extra={}):
                late = Bu is not None and A is not None and A[0] == Bu[0]
                v = u - 1

                def key_mask(c):
                    pool.wait_ge(act_kf, 4 * u + c + 1)
                    if c == 0:
                        pool.wait_ge(pool_madd, u + 1)
                    tt(kf[:, c, :], kf[:, c, :], madd[:, :], ALU.add).then_inc(pool_km, 1)

                def key_norm(c):
                    if c == 0:
                        n = count(pool, u + 1)
                        pool.wait_ge(pool_const, 4)
                        pool.wait_ge(dve_ksum, n)
                    pool.tensor_scalar(kf[:, c, :], kf[:, c, :], rk[:, c:c + 1], PS, ALU.mult, ALU.mult).then_inc(pool_kn, 1)

                def query_shift(t):
                    pool.wait_ge(dve_qmax, 4 * u + t + 1)
                    tt(heads(qf[:, t, :], A[0]), heads(qf[:, t, :], A[0]), per_head(nqmax[:, t], A[0]), ALU.add).then_inc(pool_qs, 1)

                def query_norm(t):
                    pool.wait_ge(dve_rq, 4 * u + t + 1)
                    pool.wait_ge(act_qe, 4 * u + t + 1)
                    tt(heads(qf[:, t, :], A[0]), heads(qf[:, t, :], A[0]), per_head(rq[:, t], A[0]), ALU.mult).then_inc(pool_qn, 1)

                def h_lo(c):
                    pool.wait_ge(act_hhi, 4 * v + c + 1)
                    tt(hT[:, LO, c, :], zc(c), hT[:, HI, c, :], ALU.subtract).then_inc(pool_hlo, 1)

                def y_std(t):
                    pool.wait_ge(dve_yvar, 4 * v + t + 1)
                    tt(yr_std[:, t:t + 1], yvar[:, t:t + 1], mhalf[:, 0:1], ALU.pow).then_inc(pool_ystd, 1)

                if A:
                    if A[0] == 0:
                        pool.wait_ge(s_x, 16 * (A[1] + 1))
                    if Bu is None:
                        pool.wait_ge(s_bc, 16 * 6)
                    if reused(u, 2) and not late:
                        pool.wait_ge(dve_o, 4 * v)
                    key_mask(0)
                    if not late:
                        residual(u, *A, 0)
                        residual(u, *A, 1)
                    if "attention" in extra:
                        extra["attention"]()
                    key_mask(1)
                if Bu:
                    y_std(0)
                if A:
                    if not late:
                        residual(u, *A, 2)
                    key_mask(2)
                if Bu:
                    y_std(1)
                if A:
                    if N:
                        x_std(u + 1)
                    key_mask(3)
                if Bu:
                    y_std(2)
                if A:
                    if not late:
                        residual(u, *A, 3)
                if "keys" in extra:
                    extra["keys"]()
                if Bu:
                    y_std(3)
                if A:
                    if Bu is None:
                        pool.wait_ge(dve_prep, 1)
                    else:
                        pool.wait_ge(dve_prep, A[0] + 1)
                        pool.wait_ge(act_vhi, 4 * u)
                        pool.wait_ge(dve_vlo, 4 * u)
                    pool.tensor_copy(vms[:, :], tab[A[0]][:, bass.ds(A[1], 1), 0:4].rearrange("p a c -> p (a c)")).then_inc(pool_vm, 1)
                if Bu:
                    pool.wait_ge(dve_film, Bu[0] + 1)
                    if reused(u, 2):
                        pool.wait_ge(act_z, 4 * v)
                    pool.tensor_copy(ghs[:, :], tab[Bu[0]][:, bass.ds(Bu[1], 1), 4:12].rearrange("p a c -> p (a c)")).then_inc(pool_gh, 1)
                if A:
                    query_shift(0)
                    key_norm(0)
                    key_norm(1)
                    query_shift(1)
                    key_norm(2)
                    query_norm(0)
                    query_shift(2)
                    key_norm(3)
                    query_norm(1)
                    query_shift(3)
                if Bu:
                    h_lo(0)
                    h_lo(1)
                if A:
                    query_norm(2)
                    query_norm(3)
                if Bu:
                    h_lo(2)
                    h_lo(3)
                if A:
                    if N:
                        mask_add(u + 1, N[0])
                    if "values" in extra:
                        extra["values"]()
                    if "outputs" in extra:
                        extra["outputs"]()
                    if late:
                        pool.wait_ge(dve_o, 4 * u)
                        for t in range(NT):
                            residual(u, *A, t)

            x_std(0)
            bound(0, WK)
            mask_add(0, 0)
            bound(0, WQ)
            bound(0, WV)

            def more_bounds():
                bound(0, WO)
                weight_lo(0, WO)
                bound(1, WK)
                bound(1, WQ)

            def output_weights():
                bound(1, WO)
                pool.wait_ge(dve_h, 4)
                weight_lo(1, WO)

            step(0, (0, 0), None, None, {"keys": more_bounds})
            weight_lo(1, WK)
            weight_lo(1, WQ)
            prepare(1, 0, 1)
            bound(1, WV)
            weight_lo(1, WV)
            step(1, (0, 1), (0, 0), None, {"attention": lambda: bound(0, FILM), "values": output_weights,
                                           "outputs": lambda: x_std(2)})
            mask_add(2, 1)
            bound(1, FILM)
            pool.wait_ge(pe_film, 8)
            with pool.Fori(1, B - 1) as i:
                step(2 * i, (1, i - 1), (0, i), (0, i + 1))
                step(2 * i + 1, (0, i + 1), (1, i - 1), (1, i))
            step(30, (1, 14), (0, 15), None)
            prepare(31, 1, 15)
            step(31, (1, 15), (1, 14), None)
            step(32, None, (1, 15), None)

        @block.scalar
        def _(act):
            def split_weights(L, ms):
                for m in ms:
                    act.wait_ge(dve_scale, 4 * L + m + 1)
                    if L == 1:
                        act.wait_ge(pe_bias, min(m + 1, 3))
                        wait_split(act, 0, m)
                    for k in range(NC):
                        last = nc.scalar.activation(wsp[L][:, m, HI, k, :], wraw(L, m)[:, k, :], ACT.Copy, scale=gs[:, m, k:k + 1])
                    last.then_inc(act_whi, 1)

            def prepare(u):
                for j in range(NC):
                    act.wait_ge(pe_xt, 4 * u + j + 1)
                    if j == 0 and reused(u, 1):
                        act.wait_ge(pe_v, 4 * u)
                    nc.scalar.activation(xT[:, HI, j, :], ps[:, TR + j % 2, :], ACT.Copy).then_inc(act_xhi, 1)

            def step(u, A, Bu, N, extra={}):
                v = u - 1

                def keys(c):
                    act.wait_ge(pe_k, 4 * u + c + 1)
                    if c == 0:
                        act.wait_ge(dve_keys, A[0] + 1)
                        if A[0] == 0:
                            act.wait_ge(dve_kb, A[1] + 1)
                        if Bu:
                            act.wait_ge(pe_kt, 4 * u)
                    bias = kbias if A[0] == 0 else bkp[:, 1]
                    nc.scalar.activation(kf[:, c, :], ps[:, PROJ + c % 3, :], ACT.Identity, bias=bias[:, c:c + 1],
                                         scale=c1(A[0], CK)).then_inc(act_kf, 1)

                def key_exp(c):
                    act.wait_ge(dve_kmax, 4 * u + c + 1)
                    nc.scalar.activation(kf[:, c, :], kf[:, c, :], ACT.Exp, bias=nkmax[:, c:c + 1],
                                         accum_out=ksum[:, c:c + 1]).then_inc(act_ke, 1)

                def y_norm(t):
                    act.wait_ge(dve_ynb, 4 * v + t + 1)
                    if t == 0 and reused(u, 2):
                        act.wait_ge(pe_yt, 4 * v)
                    elif t == 0:
                        wait_split(act, 1, WV)
                    nc.scalar.activation(yh[:, t, :], ps[:, TAIL + (1 + t) % 3, :], ACT.Identity, bias=ynb[:, t:t + 1],
                                         scale=yr_std[:, t:t + 1]).then_inc(act_yh, 1)

                def query_exp(t):
                    act.wait_ge(pool_qs, 4 * u + t + 1)
                    nc.scalar.activation(qf[:, t, :], qf[:, t, :], ACT.Exp).then_inc(act_qe, 1)

                def film_in(c):
                    act.wait_ge(pe_yt, 4 * v + c + 1)
                    if c == 0:
                        act.wait_ge(pool_gh, v + 1)
                    if reused(u, 2):
                        act.wait_ge(pool_hlo, 4 * v)
                    nc.scalar.activation(zc(c), ps[:, TR + c % 2, :], ACT.Identity, bias=ghs[:, 4 + c:5 + c],
                                         scale=ghs[:, c:c + 1]).then_inc(act_z, 1)

                def tanh(c):
                    act.wait_ge(act_z, 4 * v + c + 1)
                    if c >= 2 or reused(u, 2):
                        act.wait_ge(dve_h, 4 * v + c - 1)
                    else:
                        wait_split(act, 1, WV)
                    nc.scalar.activation(th[:, c % 2, :], zc(c), ACT.Tanh, scale=c1(Bu[0], INV + FILM)).then_inc(act_th, 1)

                def h_hi(c):
                    act.wait_ge(dve_h, 4 * v + c + 1)
                    if c == 0 and reused(u, 2):
                        act.wait_ge(pe_o, 4 * v)
                    nc.scalar.activation(hT[:, HI, c, :], zc(c), ACT.Copy).then_inc(act_hhi, 1)

                def k_hi(t):
                    act.wait_ge(pe_kt, 4 * u + t + 1)
                    nc.scalar.activation(Ks[:, HI, t, :], ps[:, TR + t % 2, :], ACT.Copy).then_inc(act_khi, 1)

                def v_hi(t):
                    act.wait_ge(dve_v, 4 * u + t + 1)
                    if t == 0:
                        act.wait_ge(pool_vm, u + 1)
                        if Bu:
                            act.wait_ge(pe_at, u)
                    nc.scalar.activation(Vs[:, HI, t, :], vtmp[:, t % 2, :], ACT.Copy, scale=vms[:, t:t + 1]).then_inc(act_vhi, 1)

                def q_hi(c):
                    act.wait_ge(pe_qt, 4 * u + c + 1)
                    if c == 0 and Bu:
                        act.wait_ge(pe_y, 4 * u)
                    nc.scalar.activation(qT[:, HI, c, :], ps[:, TR + c % 2, :], ACT.Copy, scale=PS).then_inc(act_qhi, 1)

                if A:
                    keys(0)
                if Bu:
                    act.wait_ge(dve_af, v + 1)
                    if reused(u, 2):
                        act.wait_ge(pe_y, 4 * v)
                    nc.scalar.activation(As[:, HI, :], af[:, :], ACT.Copy).then_inc(act_ahi, 1)
                if A:
                    key_exp(0)
                    keys(1)
                    key_exp(1)
                    keys(2)
                if Bu:
                    y_norm(0)
                if A:
                    key_exp(2)
                    keys(3)
                if Bu:
                    y_norm(1)
                    y_norm(2)
                if A:
                    key_exp(3)
                if "keys" in extra:
                    extra["keys"]()
                if Bu:
                    y_norm(3)
                if A:
                    query_exp(0)
                    query_exp(1)
                if Bu:
                    film_in(0)
                    film_in(1)
                if A:
                    query_exp(2)
                if Bu:
                    tanh(0)
                    tanh(1)
                    film_in(2)
                    film_in(3)
                if A:
                    query_exp(3)
                if Bu:
                    h_hi(0)
                    h_hi(1)
                if A:
                    v_hi(0)
                if A:
                    k_hi(0)
                    k_hi(1)
                    v_hi(1)
                if Bu:
                    tanh(2)
                    tanh(3)
                if A:
                    k_hi(2)
                    k_hi(3)
                if Bu:
                    h_hi(2)
                    h_hi(3)
                if A:
                    v_hi(2)
                    q_hi(0)
                    q_hi(1)
                    v_hi(3)
                    if "values" in extra:
                        extra["values"]()
                    q_hi(2)
                    q_hi(3)
                    if N:
                        prepare(u + 1)

            act.wait_ge(s_small, 48)
            nc.scalar.activation(th[0:B, :, :].rearrange("p a n -> p (a n)"), z[0:B, 0:2, :].rearrange("p a n -> p (a n)"),
                                 ACT.Tanh, scale=0.5).then_inc(act_pro, 1)
            prepare(0)
            split_weights(0, (WK, WQ))

            def film_copy(n, quarters):
                for q, columns in quarters:
                    act.wait_ge(pe_film, n)
                    nc.scalar.activation(film_place(z, q, columns), film_place(ps[:, TAIL:TAIL + 2, :], q, columns),
                                         ACT.Copy).then_inc(act_fcopy, 1)

            def more_weights():
                split_weights(0, (WV, WO))
                film_copy(4, ((0, 512), (2, 512)))
                split_weights(1, (WK, WQ))

            def half_film():
                act.wait_ge(pool_hlo, 4)
                film_copy(6, ((0, 512),))
                split_weights(1, (WO,))

            step(0, (0, 0), None, None, {"keys": more_weights})
            prepare(1)
            split_weights(1, (WV,))
            step(1, (0, 1), (0, 0), None, {"values": half_film})
            film_copy(8, ((2, 512),))
            prepare(2)
            wait_split(act, 1, WO)
            with act.Fori(1, B - 1) as i:
                step(2 * i, (1, i - 1), (0, i), (0, i + 1))
                step(2 * i + 1, (0, i + 1), (1, i - 1), (1, i))
            step(30, (1, 14), (0, 15), None)
            prepare(31)
            step(31, (1, 15), (1, 14), None)
            step(32, None, (1, 15), None)

        @block.vector
        def _(dve):
            ts, stt, tt = nc.vector.tensor_scalar, nc.vector.scalar_tensor_tensor, nc.vector.tensor_tensor
            steps = [0]

            def link(ins):
                steps[0] += 1
                ins.then_inc(dve_pro, 1)
                dve.wait_ge(dve_pro, steps[0])

            def power(L, src, j):
                bits = c1(L, TMP).bitcast(I32)
                link(ts(c1(L, TMP), src, 2.0 ** -20, None, ALU.max))
                link(ts(bits, bits, 0x7F800000, None, ALU.bitwise_and))
                link(ts(c1(L, S + j).bitcast(I32), bits, -1.0, float(268 << 23), ALU.mult, ALU.add))
                link(ts(c1(L, INV + j).bitcast(I32), bits, float(14 << 23), None, ALU.subtract))

            def weight_bound(L, m):
                if L == 0:
                    dve.wait_ge(s_w0[m], 16)
                else:
                    dve.wait_ge(s_stage[WEIGHT_STAGE[m]], 16 * WEIGHT_LOAD[m])
                if 4 * L + m > 0:
                    dve.wait_ge(dve_am, 4 * L + m)
                link(nc.vector.tensor_reduce(kam[:, 0, :], wraw(L, m), AX.X, ALU.max, apply_absolute_value=True))
                if m != WO:
                    link(tt(kam[:, 0, :], kam[:, 0, :], gabs[:, :], ALU.mult))
                nc.vector.reduce_max(c1(L, AM + m), kam[:, 0, :], AX.X).then_inc(dve_am, 1)

            def weight_scale(L, m):
                dve.wait_ge(pool_am, 4 * L + m + 1)
                power(L, c1(L, AR + m), m)
                if L == 1:
                    dve.wait_ge(act_whi, m + 1)
                    wait_split(dve, 0, m)
                if m != WO:
                    ins = ts(gs[:, m, :], cols[:, NV * L + G:NV * L + G + NC], c1(L, S + m), None, ALU.mult)
                else:
                    ins = ts(gs[:, m, :], ident[:, 0:NC], 0.0, c1(L, S + m), ALU.mult, ALU.add)
                ins.then_inc(dve_scale, 1)

            def weight_lo(L, m):
                dve.wait_ge(dve_scale, 4 * L + m + 1)
                dve.wait_ge(act_whi, 4 * L + m + 1)
                for k in range(NC):
                    ins = stt(wsp[L][:, m, LO, k, :], wraw(L, m)[:, k, :], gs[:, m, k:k + 1], wsp[L][:, m, HI, k, :],
                              ALU.mult, ALU.subtract)
                ins.then_inc(dve_wlo, 1)

            def key_constants(L):
                dve.wait_ge(pe_bias, 3 * L + 1)
                link(tt(bkp[:, L, :], ps[:, TAIL, 0:NC], cols[:, NV * L + BK:NV * L + BK + NC], ALU.add))
                ts(c1(L, CK), c1(L, INV + WK), 1.0 / XS, None, ALU.mult).then_inc(dve_keys, 1)

            def query_constants(L):
                dve.wait_ge(pe_bias, 3 * L + 2)
                dve.wait_ge(s_bc, 16 * 6)
                link(tt(bc[L][:, 0, :], ps[:, TAIL + 1, :], bc[L][:, 0, :], ALU.add))
                ts(c1(L, CQ), c1(L, INV + WQ), 1.0 / XS, None, ALU.mult).then_inc(dve_biasq, 1)
                dve.wait_ge(dve_biasq, L + 1)

            def value_constants(L):
                dve.wait_ge(pe_bias, 3 * L + 3)
                link(tt(bc[L][:, 1, :], ps[:, TAIL + 2, :], bc[L][:, 1, :], ALU.add))
                link(ts(c1(L, CV), c1(L, INV + WV), 1.0 / XS, None, ALU.mult))
                link(nc.vector.tensor_reduce(c1(L, TMP + 1), bc[L][:, 1, :], AX.X, ALU.max, apply_absolute_value=True))
                link(stt(c1(L, TMP + 1), c1(L, AR + WV), float(D), c1(L, TMP + 1), ALU.mult, ALU.add))
                power(L, c1(L, TMP + 1), VAL)
                link(ts(c1(L, TMP + 2), c1(L, S + VAL), PS, None, ALU.mult))
                link(tt(c1(L, TMP + 2), c1(L, TMP + 2), c1(L, TMP + 2), ALU.mult))
                link(ts(c1(L, EPSY), c1(L, TMP + 2), EPS, None, ALU.mult))
                link(ts(tab[L][:, :, 0:NT], tab[L][:, :, 0:NT], c1(L, S + VAL), None, ALU.mult))
                nc.vector.tensor_copy(c1(L, TMP + 3), c1(L, EPSY)).then_inc(dve_prep, 1)

            def film_copy(L):
                dve.wait_ge(pe_ft, L + 1)
                nc.vector.tensor_copy(film_t[:, :, :, :].rearrange("p a c b -> p (a c b)"), ps[:, TAIL + 2, 0:NE * B]).then_inc(dve_fcopy, 1)

            def film(L):
                c0 = NV * L
                dve.wait_ge(dve_fcopy, L + 1)
                f = film_t[:, :, :, :].rearrange("p a c b -> p (a c) b")
                for c in range(NC):
                    nc.vector.tensor_scalar(film_t[:, 0, c, :], f[:, c, :], cols[:, c0 + BE + c:c0 + BE + c + 1], 1.0, ALU.add, ALU.add)
                    ins = ts(film_t[:, 1, c, :], f[:, NC + c, :], cols[:, c0 + BE + NC + c:c0 + BE + NC + c + 1], None, ALU.add)
                link(ins)
                for c in range(NC):
                    ts(tab[L][:, :, 4 + c], film_t[:, 0, c, :], cols[:, c0 + FS + c:c0 + FS + c + 1], 0.5, ALU.mult, ALU.mult)
                    ins = stt(film_t[:, 1, c, :], film_t[:, 0, c, :], cols[:, c0 + FB + c:c0 + FB + c + 1], film_t[:, 1, c, :], ALU.mult, ALU.add)
                link(ins)
                for c in range(NC):
                    ins = ts(tab[L][:, :, 8 + c], film_t[:, 1, c, :], 0.5, None, ALU.mult)
                link(ins)
                a, b = film_t[:, 0, :, :].rearrange("p c b -> p b c"), film_t[:, 1, :, :].rearrange("p c b -> p b c")
                gain, shift = tab[L][:, :, 4:8], tab[L][:, :, 8:12]
                link(stt(a, gain, -1.0, gain, ALU.mult, ALU.max))
                link(stt(b, shift, -1.0, shift, ALU.mult, ALU.max))
                link(ts(film_t[:, 1, :, :], film_t[:, 1, :, :], 2.0, None, ALU.mult))
                link(stt(film_t[:, 0, :, :], film_t[:, 0, :, :], 2.0 * ROOT, film_t[:, 1, :, :], ALU.mult, ALU.add))
                nc.vector.reduce_max(c1(L, AM + FILM), film_t[:, 0, :, :].rearrange("p c b -> p (c b)"), AX.X).then_inc(dve_filmam, 1)
                dve.wait_ge(pool_filmam, L + 1)
                power(L, c1(L, AR + FILM), FILM)
                link(ts(tab[L][:, :, 4:12], tab[L][:, :, 4:12], c1(L, S + FILM), None, ALU.mult))
                tt(c1(L, CO), c1(L, INV + WO), c1(L, INV + FILM), ALU.mult).then_inc(dve_film, 1)
                dve.wait_ge(dve_film, L + 1)

            def x_stats(u, L, b, t, tails):
                if tails is None:
                    dve.wait_ge(dve_o, 4 * u - 8 + t + 1)
                elif t == 0:
                    if L == 0:
                        dve.wait_ge(s_x, 16 * (b + 1))
                    else:
                        dve.wait_ge(dve_o, 4 * tails)
                nc.vector.bn_stats(xbs[:, t, :], xin[L][:, t, :]).then_inc(dve_xst, 1)

            def x_mean(u):
                for t in range(NT):
                    nc.vector.bn_aggr(xmv[:, t, :], xbs[:, t, :]).then_inc(dve_xag, 1)
                dve.wait_ge(dve_xag, 4 * u + 4)
                ts(xvar[:, :], xmv[:, :, 1], EPS, XS ** -2, ALU.add, ALU.mult).then_inc(dve_xvar, 1)

            def x_norm(u, L, t):
                if t == 0:
                    dve.wait_ge(pool_xstd, u + 1)
                    if reused(u, 1):
                        dve.wait_ge(pe_xt, 4 * u)
                ts(xh[:, t, :], xin[L][:, t, :], xmv[:, t, 0:1], xr_std[:, t:t + 1], ALU.subtract, ALU.mult).then_inc(dve_xh, 1)

            def x_lo(u, j):
                dve.wait_ge(act_xhi, 4 * u + j + 1)
                stt(xT[:, LO, j, :], ps[:, TR + j % 2, :], 1.0, xT[:, HI, j, :], ALU.mult, ALU.subtract).then_inc(dve_xlo, 1)

            def all_masked(u, b):
                dve.wait_ge(pool_madd, u + 1)
                nc.vector.reduce_max(nan0[:, 0:1], madd[:, :], AX.X).then_inc(dve_kb1, 1)
                dve.wait_ge(dve_kb1, 2 * b + 1)
                ts(nan0[:, 1:2], nan0[:, 0:1], 10.0, 0.0, ALU.mult, ALU.mult).then_inc(dve_kb1, 1)
                dve.wait_ge(dve_kb1, 2 * b + 2)
                ts(kbias[:, :], bkp[:, 0, :], nan0[:, 1:2], None, ALU.add).then_inc(dve_kb, 1)

            def step(u, A, Bu, N, extra={}):
                v = u - 1

                def key_max(c, stats=False):
                    dve.wait_ge(pool_km, 4 * u + c + 1)
                    if stats:
                        dve.wait_ge(dve_xst, 4 * u + 8)
                    nc.vector.reduce_max(nkmax[:, c:c + 1], kf[:, c, :], AX.X, negate=True).then_inc(dve_kmax, 1)

                def y_stats(t):
                    dve.wait_ge(pe_y, 4 * v + t + 1)
                    nc.vector.bn_stats(ybs[:, t, :], ps[:, TAIL + (1 + t) % 3, :]).then_inc(dve_yst, 1)
                    n = count(dve, 4 * v + t + 1)
                    dve.wait_ge(s_rows, 16 * 12)
                    dve.wait_ge(dve_yst, n)
                    nc.vector.bn_aggr(ymv[:, t, :], ybs[:, t, :]).then_inc(dve_yag, 1)
                    dve.wait_ge(dve_yag, 4 * v + t + 1)
                    ts(yvar[:, t:t + 1], ymv[:, t, 1:2], c1(Bu[0], EPSY), None, ALU.add).then_inc(dve_yvar, 1)

                def y_shift(t):
                    dve.wait_ge(pool_ystd, 4 * v + t + 1)
                    stt(ynb[:, t:t + 1], ymv[:, t, 0:1], -1.0, yr_std[:, t:t + 1], ALU.mult, ALU.mult).then_inc(dve_ynb, 1)

                def query(t):
                    dve.wait_ge(pe_q, 4 * u + t + 1)
                    if t == 0 and Bu:
                        dve.wait_ge(pe_qt, 4 * u)
                    stt(qf[:, t, :], ps[:, PROJ + (4 + t) % 3, :], c1(A[0], CQ), bc[A[0]][:, 0, :], ALU.mult, ALU.add).then_inc(dve_q, 1)
                    dve.wait_ge(dve_q, 4 * u + t + 1)
                    nc.vector.reduce_max(nqmax[:, t, 0:HEADS[A[0]]], heads(qf[:, t, :], A[0]), AX.X, negate=True).then_inc(dve_qmax, 1)

                def query_sum(t):
                    dve.wait_ge(act_qe, 4 * u + t + 1)
                    h = HEADS[A[0]]
                    nc.vector.reduce_sum(qsum[:, t, 0:h], heads(qf[:, t, :], A[0]), AX.X).then_inc(dve_qs, 1)
                    dve.wait_ge(dve_qs, 4 * u + t + 1)
                    nc.vector.reciprocal(rq[:, t, 0:h], qsum[:, t, 0:h]).then_inc(dve_rq, 1)

                def silu(c):
                    dve.wait_ge(act_th, 4 * v + c + 1)
                    stt(zc(c), th[:, c % 2, :], 1.0, zc(c), ALU.add, ALU.mult).then_inc(dve_h, 1)

                def value(t):
                    dve.wait_ge(pe_v, 4 * u + t + 1)
                    if t >= 2 or Bu:
                        dve.wait_ge(dve_vlo, 4 * u + t - 1)
                    stt(vtmp[:, t % 2, :], ps[:, PROJ + (8 + t) % 3, :], c1(A[0], CV), bc[A[0]][:, 1, :], ALU.mult, ALU.add).then_inc(dve_v, 1)

                def v_lo(t):
                    dve.wait_ge(act_vhi, 4 * u + t + 1)
                    stt(Vs[:, LO, t, :], vtmp[:, t % 2, :], vms[:, t:t + 1], Vs[:, HI, t, :], ALU.mult, ALU.subtract).then_inc(dve_vlo, 1)

                def k_lo(t):
                    dve.wait_ge(act_khi, 4 * u + t + 1)
                    stt(Ks[:, LO, t, :], ps[:, TR + t % 2, :], 1.0, Ks[:, HI, t, :], ALU.mult, ALU.subtract).then_inc(dve_klo, 1)

                def q_lo(c):
                    dve.wait_ge(act_qhi, 4 * u + c + 1)
                    stt(qT[:, LO, c, :], ps[:, TR + c % 2, :], PS, qT[:, HI, c, :], ALU.mult, ALU.subtract).then_inc(dve_qlo, 1)

                def output(t):
                    dve.wait_ge(pe_o, 4 * v + t + 1)
                    L, b = Bu
                    if t == 0:
                        dve.wait_ge(pool_xr, 4 * u + 4 if L == 0 and A and A[0] == 1 else 4 * v + 4)
                        if L == 0 and isinstance(u, int) and u == 1:
                            dve.wait_ge(pe_film, 5)
                    dst = xin[1] if L == 0 else xr[1]
                    stt(dst[:, t, :], ps[:, TAIL + (5 + t) % 3 if A else LAST[t], :], c1(L, CO), xr[L][:, t, :], ALU.mult, ALU.add).then_inc(dve_o, 1)

                if A and "attention" not in extra:
                    key_max(0)
                if Bu:
                    dve.wait_ge(pe_at, v + 1)
                    if reused(u, 2):
                        dve.wait_ge(pool_hlo, 4 * v)
                    stt(af[:, :], ps[:, TAIL, :], 1.0 / PS, diag[Bu[0]][:, :], ALU.mult, ALU.mult).then_inc(dve_af, 1)
                    dve.wait_ge(act_ahi, v + 1)
                    tt(As[:, LO, :], af[:, :], As[:, HI, :], ALU.subtract).then_inc(dve_alo, 1)
                if "attention" in extra:
                    extra["attention"]()
                    key_max(0)
                if N:
                    x_stats(u + 1, *N, 0, v)
                if Bu:
                    y_stats(0)
                if A:
                    if N:
                        x_stats(u + 1, *N, 1, v)
                    key_max(1)
                if Bu:
                    y_shift(0)
                if N:
                    x_stats(u + 1, *N, 2, v)
                    x_stats(u + 1, *N, 3, v)
                if Bu:
                    y_stats(1)
                if A:
                    key_max(2, stats=bool(N))
                if N:
                    x_mean(u + 1)
                if Bu:
                    y_shift(1)
                    y_stats(2)
                if A:
                    key_max(3)
                if Bu:
                    y_shift(2)
                if "keys" in extra:
                    extra["keys"]()
                if A:
                    query(0)
                if Bu:
                    y_stats(3)
                if A:
                    dve.wait_ge(act_ke, 4 * u + 4)
                    nc.vector.reciprocal(rk[:, :], ksum[:, :]).then_inc(dve_ksum, 1)
                if Bu:
                    y_shift(3)
                if A:
                    query(1)
                    query_sum(0)
                    query(2)
                    query_sum(1)
                    query(3)
                if A:
                    query_sum(2)
                if Bu:
                    silu(0)
                    silu(1)
                if A:
                    query_sum(3)
                    value(0)
                if A:
                    v_lo(0)
                    value(1)
                    k_lo(0)
                    k_lo(1)
                    v_lo(1)
                if Bu:
                    silu(2)
                    silu(3)
                if A:
                    value(2)
                    k_lo(2)
                    k_lo(3)
                    v_lo(2)
                    value(3)
                    q_lo(0)
                    q_lo(1)
                    v_lo(3)
                if N:
                    for t in range(NT):
                        x_norm(u + 1, N[0], t)
                if "values" in extra:
                    extra["values"]()
                if Bu:
                    output(0)
                if "stats" in extra:
                    extra["stats"](0)
                if A:
                    q_lo(2)
                    q_lo(3)
                if Bu:
                    output(1)
                if "stats" in extra:
                    extra["stats"](1)
                if N:
                    x_lo(u + 1, 0)
                    x_lo(u + 1, 1)
                if Bu:
                    output(2)
                if "stats" in extra:
                    extra["stats"](2)
                if N:
                    if N[0] == 0:
                        all_masked(u + 1, N[1])
                    x_lo(u + 1, 2)
                    x_lo(u + 1, 3)
                if Bu:
                    output(3)
                if "stats" in extra:
                    extra["stats"](3)

            def prepare(u, L, b, meanwhile=None):
                if u == 2:
                    wait_split(dve, 1, WO)
                if L == 0:
                    for t in range(NT):
                        x_stats(u, L, b, t, u - 1)
                dve.wait_ge(dve_xst, 4 * u + 4)
                x_mean(u)
                if meanwhile:
                    meanwhile()
                for t in range(NT):
                    x_norm(u, L, t)

            def x_los(u):
                for j in range(NC):
                    x_lo(u, j)

            def norm_vectors(L):
                g, b = (cols[:, NV * L + j:NV * L + j + NC] for j in (G, LNB))
                link(stt(gabs[:, :], g, -1.0, g, ALU.mult, ALU.max))
                link(nc.vector.tensor_copy(af[:, :].rearrange("p (k n) -> p k n", k=NC),
                                           b.rearrange("p (k n) -> p k n", n=1).to_broadcast((P, NC, P))))
                nc.vector.tensor_copy(c1(L, TMP + 4), gabs[:, 0:1]).then_inc(dve_bias, 1)

            def columns():
                dve.wait_ge(pe_pro, 1)
                link(nc.vector.tensor_copy(cols[:, :], ps[:, TR, 0:2 * NV]))
                norm_vectors(0)

            def condition():
                dve.wait_ge(s_small, 48)
                cond_in, tanh_in = z[0:B, 0:2, :].rearrange("p a n -> p (a n)"), th[0:B, :, :].rearrange("p a n -> p (a n)")
                dve.wait_ge(act_pro, 1)
                link(stt(cond_in, tanh_in, 1.0, cond_in, ALU.add, ALU.mult))
                link(ts(vtmp[0:B, 0, :], vtmp[0:B, 0, :].bitcast(I32), 1.0, -1.0, ALU.is_equal, ALU.mult))
                ts(vtmp[0:B, 0, :], vtmp[0:B, 0, :], 1.0, None, ALU.add).then_inc(dve_emb, 1)

            def embedding():
                dve.wait_ge(pe_pro, 2)
                link(ts(embT[:, :, :], ps[:, TR, 0:NE * B].rearrange("p (k b) -> p k b", k=NE), 0.5, None, ALU.mult))
                for L in range(2):
                    c = (NE + NT * L) * B
                    ins = nc.vector.tensor_copy(tab[L][:, :, 0:NT], ps[:, TR, c:c + NT * B].rearrange("p (t b) -> p b t", t=NT))
                    if L == 0:
                        link(ins)
                ins.then_inc(dve_emb, 1)
                dve.wait_ge(dve_emb, 2)

            def more_weights():
                query_constants(0)
                weight_bound(0, WO)
                weight_scale(0, WO)
                weight_lo(0, WV)
                value_constants(0)
                norm_vectors(1)
                weight_bound(1, WK)
                weight_scale(1, WK)
                weight_bound(1, WQ)
                weight_scale(1, WQ)

            prepare(0, 0, 0, meanwhile=columns)
            weight_bound(0, WK)
            x_lo(0, 0)
            x_lo(0, 1)
            weight_scale(0, WK)
            condition()
            x_lo(0, 2)
            x_lo(0, 3)
            weight_lo(0, WK)
            weight_bound(0, WQ)
            key_constants(0)
            dve.wait_ge(dve_keys, 1)
            all_masked(0, 0)
            weight_scale(0, WQ)
            weight_bound(0, WV)
            weight_lo(0, WQ)
            weight_scale(0, WV)
            embedding()
            step(0, (0, 0), None, None, {"keys": more_weights})
            prepare(1, 0, 1)
            film_copy(0)
            weight_bound(1, WV)
            weight_scale(1, WV)
            x_los(1)
            key_constants(1)
            query_constants(1)
            all_masked(1, 1)
            value_constants(1)

            def output_weights():
                weight_bound(1, WO)
                weight_scale(1, WO)

            step(1, (0, 1), (0, 0), None, {"attention": lambda: film(0), "values": output_weights,
                                           "stats": lambda t: x_stats(2, 1, 0, t, None)})
            prepare(2, 1, 0)
            x_los(2)
            film_copy(1)
            film(1)
            with dve.Fori(1, B - 1) as i:
                step(2 * i, (1, i - 1), (0, i), (0, i + 1))
                step(2 * i + 1, (0, i + 1), (1, i - 1), (1, i))
            step(30, (1, 14), (0, 15), None, {"stats": lambda t: x_stats(31, 1, 15, t, None)})
            prepare(31, 1, 15)
            x_los(31)
            step(31, (1, 15), (1, 14), None)
            step(32, None, (1, 15), None)

        @block.tensor
        def _(pe):
            mm = nc.tensor.matmul

            def prepare(u):
                for j in range(NC):
                    x_transpose(u, j)

            def x_transpose(u, j):
                if j == 0:
                    pe.wait_ge(dve_xh, 4 * u + 4)
                if j >= 2:
                    pe.wait_ge(dve_xlo, 4 * u + j - 1)
                elif reused(u, 1):
                    pe.wait_ge(dve_qlo, 4 * u - 1 + j)
                for t in range(NT):
                    last = nc.tensor.transpose(ps[:, TR + j % 2, P * t:P * t + P], xh[:, t, P * j:P * j + P], ident[:, :])
                last.then_inc(pe_xt, 1)

            def bias(L, ms):
                for m in ms:
                    if L == 0:
                        pe.wait_ge(s_w0[m], 16)
                    else:
                        pe.wait_ge(s_stage[WEIGHT_STAGE[m]], 16 * WEIGHT_LOAD[m])
                    pe.wait_ge(dve_bias, L + 1)
                    W = wraw(L, m)
                    if m == WK:
                        for c in range(NC):
                            for k in range(NC):
                                last = mm(ps[:, TAIL, c:c + 1], W[:, k, P * c:P * c + P], af[:, P * k:P * k + 1],
                                          start=(k == 0), stop=(k == NC - 1))
                    else:
                        for k in range(NC):
                            last = mm(ps[:, TAIL + m, :], af[:, P * k:P * k + P], W[:, k, :], start=(k == 0), stop=(k == NC - 1))
                    last.then_inc(pe_bias, 1)

            def film(L, quarters):
                pe.wait_ge(dve_biasq, L + 1)
                for q in quarters:
                    pe.wait_ge(s_stage[FILM_STAGE[L][q]], 16 * FILM_LOAD[L][q])
                    for k in range(NE):
                        last = mm(film_place(ps[:, TAIL:TAIL + 2, :], q, 256), embT[:, k, :], quarter(L, q)[:, k, :],
                                  start=(k == 0), stop=(k == NE - 1))
                    last.then_inc(pe_film, 1)

            def film_transpose(L):
                pe.wait_ge(act_fcopy, 2 + 2 * L)
                for c in range(NE):
                    last = nc.tensor.transpose(ps[:, TAIL + 2, B * c:B * c + B], z[0:B, c // 4, P * (c % 4):P * (c % 4) + P], ident[0:B, 0:B])
                last.then_inc(pe_ft, 1)

            def step(u, A, Bu, N, extra={}):
                v = u - 1

                def product(bank, stationary, moving):
                    n = 0
                    for a, b in PRODUCTS:
                        for k in range(NC):
                            last = mm(ps[:, bank, :], stationary(a, k), moving(b, k), start=(n == 0), stop=(n == 11))
                            n += 1
                    return last

                def keys(c):
                    if c == 0:
                        pe.wait_ge(dve_xlo, 4 * u + 4)
                        wait_split(pe, A[0], WK)
                    if c < 3:
                        if Bu:
                            pe.wait_ge(dve_v, 4 * u - 2 + c)
                    else:
                        pe.wait_ge(act_kf, 4 * u + 1)
                    W = wsp[A[0]][:, WK]
                    product(PROJ + c % 3, lambda a, k: W[:, a, k, P * c:P * c + P], lambda b, k: xT[:, b, k, :]).then_inc(pe_k, 1)

                def queries(t):
                    if t < 3:
                        pe.wait_ge(act_kf, 4 * u + t + 2)
                    else:
                        pe.wait_ge(dve_q, 4 * u + 1)
                    if t == 0:
                        wait_split(pe, A[0], WQ)
                    W = wsp[A[0]][:, WQ]
                    product(PROJ + (4 + t) % 3, lambda a, k: xT[:, a, k, P * t:P * t + P], lambda b, k: W[:, b, k, :]).then_inc(pe_q, 1)

                def values(t):
                    if t < 3:
                        pe.wait_ge(dve_q, 4 * u + t + 2)
                    else:
                        pe.wait_ge(dve_v, 4 * u + 1)
                    if t == 0:
                        wait_split(pe, A[0], WV)
                    W = wsp[A[0]][:, WV]
                    product(PROJ + (8 + t) % 3, lambda a, k: xT[:, a, k, P * t:P * t + P], lambda b, k: W[:, b, k, :]).then_inc(pe_v, 1)

                def attention():
                    pe.wait_ge(dve_vlo, 4 * v + 4)
                    pe.wait_ge(dve_klo, 4 * v + 4)
                    if reused(u, 2):
                        pe.wait_ge(dve_o, 4 * v - 2)
                    else:
                        pe.wait_ge(dve_keys, 2)
                    st, mv = (Vs, Ks) if Bu[0] == 0 else (Ks, Vs)
                    for c in range(NC):
                        n = 0
                        for a, b in PRODUCTS:
                            for t in range(NT):
                                last = mm(ps[:, TAIL, P * c:P * c + P], st[:, a, t, P * c:P * c + P], mv[:, b, t, P * c:P * c + P],
                                          start=(n == 0), stop=(n == 11))
                                n += 1
                    last.then_inc(pe_at, 1)

                def ys(t):
                    if t == 0:
                        pe.wait_ge(dve_qlo, 4 * v + 4)
                        pe.wait_ge(dve_alo, v + 1)
                    if t < 2:
                        if reused(u, 2):
                            pe.wait_ge(dve_o, 4 * v - 1 + t)
                        elif t == 0:
                            pe.wait_ge(dve_prep, 2)
                    elif t == 3:
                        pe.wait_ge(act_yh, 4 * v + 1)
                    for c in range(NC):
                        for n, (a, b) in enumerate(PRODUCTS):
                            last = mm(ps[:, TAIL + (1 + t) % 3, P * c:P * c + P], qT[:, a, c, P * t:P * t + P], As[:, b, P * c:P * c + P],
                                      start=(n == 0), stop=(n == 2))
                    last.then_inc(pe_y, 1)

                def y_transpose(c):
                    if c == 0:
                        pe.wait_ge(act_yh, 4 * v + 4)
                    if c < 2:
                        if not A:
                            pe.wait_ge(dve_qlo, 4 * v + 3 + c)
                    else:
                        pe.wait_ge(act_z, 4 * v + c - 1)
                    for t in range(NT):
                        last = nc.tensor.transpose(ps[:, TR + c % 2, P * t:P * t + P], yh[:, t, P * c:P * c + P], ident[:, :])
                    last.then_inc(pe_yt, 1)

                def k_transpose(t):
                    if t == 0:
                        pe.wait_ge(pool_kn, 4 * u + 4)
                    if t >= 2:
                        pe.wait_ge(dve_klo, 4 * u + t - 1)
                    elif Bu:
                        pe.wait_ge(act_z, 4 * v + 3 + t)
                    for c in range(NC):
                        last = nc.tensor.transpose(ps[:, TR + t % 2, P * c:P * c + P], kf[:, c, P * t:P * t + P], ident[:, :])
                    last.then_inc(pe_kt, 1)

                def q_transpose(c):
                    if c == 0:
                        pe.wait_ge(pool_qn, 4 * u + 4)
                    if c >= 2:
                        pe.wait_ge(dve_qlo, 4 * u + c - 1)
                    else:
                        pe.wait_ge(dve_klo, 4 * u + 3 + c)
                    for t in range(NT):
                        last = nc.tensor.transpose(ps[:, TR + c % 2, P * t:P * t + P], qf[:, t, P * c:P * c + P], ident[:, :])
                    last.then_inc(pe_qt, 1)

                def output(t):
                    if t == 0:
                        pe.wait_ge(pool_hlo, 4 * v + 4)
                        wait_split(pe, Bu[0], WO)
                    if t < 3:
                        pe.wait_ge(act_yh, 4 * v + t + 2)
                    else:
                        pe.wait_ge(dve_o, 4 * v + 1)
                    W = wsp[Bu[0]][:, WO]
                    product(TAIL + (5 + t) % 3, lambda a, k: hT[:, a, k, P * t:P * t + P], lambda b, k: W[:, b, k, :]).then_inc(pe_o, 1)

                if A:
                    keys(0)
                if Bu:
                    attention()
                if A:
                    keys(1)
                if Bu:
                    ys(0)
                if A:
                    keys(2)
                if Bu:
                    ys(1)
                if A:
                    keys(3)
                if Bu:
                    ys(2)
                if "keys" in extra:
                    extra["keys"]()
                if A:
                    queries(0)
                if Bu:
                    ys(3)
                if A:
                    queries(1)
                    queries(2)
                if Bu:
                    y_transpose(0)
                    y_transpose(1)
                if A:
                    queries(3)
                if Bu:
                    y_transpose(2)
                    y_transpose(3)
                if A:
                    values(0)
                    values(1)
                    k_transpose(0)
                    k_transpose(1)
                    values(2)
                    k_transpose(2)
                    k_transpose(3)
                    values(3)
                    q_transpose(0)
                    q_transpose(1)
                if "values" in extra:
                    extra["values"]()
                if not A:
                    return
                if Bu:
                    output(0)
                q_transpose(2)
                q_transpose(3)
                if Bu:
                    output(1)
                if N:
                    x_transpose(u + 1, 0)
                    x_transpose(u + 1, 1)
                if Bu:
                    output(2)
                if N:
                    x_transpose(u + 1, 2)
                    x_transpose(u + 1, 3)
                if Bu:
                    output(3)

            def last_outputs(v, L):
                W = wsp[L][:, WO]
                for k in range(NC):
                    pe.wait_ge(pool_hlo, 4 * v + k + 1)
                    if k == 0:
                        wait_split(pe, L, WO)
                        pe.wait_ge(act_yh, 4 * v + 4)
                    for n, (a, b) in enumerate(PRODUCTS):
                        for t in range(NT):
                            bank = LAST[t]
                            last = mm(ps[:, bank, :], hT[:, a, k, P * t:P * t + P], W[:, b, k, :],
                                      start=(k == 0 and n == 0), stop=(k == NC - 1 and n == 2))
                            if k == NC - 1 and n == 2:
                                last.then_inc(pe_o, 1)

            pe.wait_ge(pool_const, 5)
            pe.wait_ge(s_rows, 16 * 12)
            nc.tensor.transpose(ps[:, TR, 0:2 * NV], rows[:, :], ident[0:2 * NV, 0:2 * NV]).then_inc(pe_pro, 1)
            pe.wait_ge(dve_bias, 1)
            prepare(0)
            bias(0, (WK,))
            pe.wait_ge(dve_xlo, 3)
            pe.wait_ge(dve_emb, 1)
            for k in range(NE):
                nc.tensor.transpose(ps[:, TR, B * k:B * k + B], z[0:B, k // 4, P * (k % 4):P * (k % 4) + P], ident[0:B, 0:B])
            for L in range(2):
                for t in range(NT):
                    c = (NE + NT * L + t) * B
                    last = nc.tensor.transpose(ps[:, TR, c:c + B], vtmp[0:B, L, P * t:P * t + P], ident[0:B, 0:B])
            last.then_inc(pe_pro, 1)

            def more_products():
                bias(0, (WQ, WV))
                pe.wait_ge(dve_emb, 2)
                film(0, range(4))

            def film_transposed():
                pe.wait_ge(dve_prep, 1)
                film_transpose(0)

            step(0, (0, 0), None, None, {"keys": more_products, "values": film_transposed})
            pe.wait_ge(dve_bias, 2)
            bias(1, (WK, WQ))
            prepare(1)
            pe.wait_ge(dve_fcopy, 1)
            bias(1, (WV,))

            def half_film():
                pe.wait_ge(act_yh, 4)
                film(1, (1, 0))
                pe.wait_ge(act_fcopy, 3)

            step(1, (0, 1), (0, 0), None, {"values": half_film})
            pe.wait_ge(dve_o, 3)
            film(1, (2, 3))
            prepare(2)
            pe.wait_ge(dve_o, 4)
            film_transpose(1)
            pe.wait_ge(dve_fcopy, 2)
            with pe.Fori(1, B - 1) as i:
                step(2 * i, (1, i - 1), (0, i), (0, i + 1))
                step(2 * i + 1, (0, i + 1), (1, i - 1), (1, i))
            step(30, (1, 14), (0, 15), None)
            prepare(31)
            step(31, (1, 15), (1, 14), None)
            step(32, None, (1, 15), None)
            last_outputs(31, 1)


_W = [[f"L0_cond_{n}" for n in ("Wk", "Wq", "Wv", "film_out_W", "film_emb_W")],
      [f"L1_cond_{n}" for n in ("Wk", "Wq", "Wv", "W_out", "W_emb")]]
_VEC = [dict(g="norm_scale", lnb="norm_bias", fs="film_norm_scale", fb="film_norm_bias", bk="bk", be="film_emb_b", bq="bq", bv="bv",
             bo="film_out_b"),
        dict(g="ln_w", lnb="ln_b", fs="ln2_w", fb="ln2_b", bk="bk", be="b_emb", bq="bq", bv="bv", bo="b_out")]


def kernel(**inputs):
    import numpy as _np
    import concourse.bacc as _bacc
    from concourse import mybir as _mybir
    from concourse.bass_utils import run_bass_kernel_spmd as _run

    nc = _bacc.Bacc("TRN2", target_bir_lowering=False, num_devices=1)
    arrays = {}

    def dram(name, shape=None):
        a = _np.ascontiguousarray(inputs[name])
        if shape:
            a = a.reshape(shape)
        arrays[f"in_{name}"] = a
        return nc.dram_tensor(f"in_{name}", a.shape, _mybir.dt.from_np(a.dtype), kind="ExternalInput").ap()

    x, cond = dram("x"), dram("cond_2048")
    mask0, mask1 = dram("mask_BxS_ik0"), dram("mask_BxSx1_fk1", (B, T))
    w = [[dram(n) for n in names] for names in _W]
    vec = [{k: dram(f"L{L}_cond_{n}") for k, n in names.items()} for L, names in enumerate(_VEC)]
    out = nc.dram_tensor("out_0", (B, T, D), F32, kind="ExternalOutput").ap()
    build(nc, x, cond, mask0, mask1, w, vec, out)
    r = _run(nc, [arrays], core_ids=[0])
    return r.results[0]["out_0"]
```
